# Optimizing a Trainium2 kernel written in Bass

```python
import numpy as np
import jax
import jax.numpy as jnp

def _softmax(x, axis=-1):
    return jax.nn.softmax(x, axis=axis)

def _gelu(x):
    return jax.nn.gelu(x, approximate=True)

def _silu(x):
    return jax.nn.silu(x)

def _sigmoid(x):
    return jax.nn.sigmoid(x)

def _layernorm(x, axis=-1, eps=1e-05):
    m = jnp.mean(x, axis=axis, keepdims=True)
    v = jnp.var(x, axis=axis, keepdims=True)
    return (x - m) / jnp.sqrt(v + eps)

def _scatter_add(tgt, idx, src, axis=0):
    return tgt.at[idx].add(src)

def _segment_sum(src, seg, n):
    return jax.ops.segment_sum(src, seg, n)
kernel_name = 'mk_perceiver_d1_seqx_r2_d1eaac'

def setup_inputs(seed: int=0):
    np.random.seed(seed)
    _w = jnp.asarray

    def _rec_inputs():
        import jax
        import jax.numpy as jnp
        _rk = jax.random.key(seed)
        x = -0.0005207 + 1.001 * jax.random.normal(jax.random.fold_in(_rk, 1), (64, 32, 512), jnp.float32)
        _lenS = 32 - jax.random.randint(jax.random.fold_in(_rk, 7), (64,), 0, max(1, 32 // 4) + 1, jnp.int32)
        _lenS2 = 257 - jax.random.randint(jax.random.fold_in(_rk, 8), (64,), 0, max(1, 257 // 4) + 1, jnp.int32)
        _ctx_1024P = jax.random.normal(jax.random.fold_in(_rk, 11), (64, 16, 512), jnp.float32)
        _ctx_1024c = jax.random.dirichlet(jax.random.fold_in(_rk, 511), 0.3 * jnp.ones((16,), jnp.float32), (64, 257))
        _ctx_1024t = jnp.einsum('bsk,bkd->bsd', _ctx_1024c, _ctx_1024P)
        _ctx_1024t = _ctx_1024t * jax.lax.rsqrt(jnp.mean(jnp.square(_ctx_1024t)) + 1e-12) * 0.953939
        ctx_1024 = 4.13588e-05 + 0.999923 * (_ctx_1024t + 0.3 * jax.random.normal(jax.random.fold_in(_rk, 611), (64, 257, 512), jnp.float32))
        return (x, ctx_1024)
    x, ctx_1024 = _rec_inputs()

    def _L0_xattn_setup():
        import jax, jax.numpy as jnp
        import numpy as np
        key = jax.random.key(seed)
        k1, k2, k3 = jax.random.split(key, 3)
        B, N_LAT, N_CTX, D_MODEL = (2, 512, 2048, 512)
        x = jax.random.normal(k1, (B, N_LAT, D_MODEL), dtype=jnp.float32)
        context = jax.random.normal(k2, (B, N_CTX, D_MODEL), dtype=jnp.float32)
        W_out = jax.random.normal(k3, (D_MODEL, D_MODEL), dtype=jnp.float32) * D_MODEL ** (-0.5)
        b_out = jnp.zeros((D_MODEL,), dtype=jnp.float32)
        return {'x': x, 'context': context, 'W_out': W_out, 'b_out': b_out, 'heads': 16}
    _L0_xattn_all = _L0_xattn_setup()
    _L0_xattn_in = {k: v for k, v in _L0_xattn_all.items() if k in ('W_out', 'b_out')}
    del _L0_xattn_all

    def _L0_attn_setup():
        import jax, jax.numpy as jnp
        import numpy as np
        NUM_HEAD = 16
        D_Q = 256
        D_KV = 256
        ROPE_BASE = 10000.0

        def _cos_sin(seq_len, dim):
            pos = jnp.arange(seq_len, dtype=jnp.float32)[:, None]
            ids = jnp.arange(dim // 2, dtype=jnp.float32)
            theta = ROPE_BASE ** (-2.0 * ids) / (dim // 2)
            r = pos * theta[None, :]
            return (jnp.cos(r), jnp.sin(r))

        def _rope(x, cos, sin):
            b, s, d = x.shape
            xv = x.reshape(b, s, d // 2, 2)
            x0, x1 = (xv[..., 0], xv[..., 1])
            out = jnp.stack([x0 * cos - x1 * sin, x1 * cos + x0 * sin], axis=-1)
            return out.reshape(b, s, d)
        key = jax.random.key(seed)
        ks = jax.random.split(key, 10)
        d_model, d_q, d_kv = (512, D_Q, D_KV)
        b, s = (2, 1024)
        w = lambda k, i, o: jax.random.normal(k, (i, o), dtype=jnp.float32) * 0.02
        return {'x': jax.random.normal(ks[0], (b, s, d_model), dtype=jnp.float32), 'Wd_q_w': w(ks[1], d_model, d_q), 'Wd_q_b': jnp.zeros((d_q,), jnp.float32), 'Wu_q_w': w(ks[2], d_q, d_model), 'Wu_q_b': jnp.zeros((d_model,), jnp.float32), 'Wq_r_w': w(ks[3], d_q, d_model), 'Wq_r_b': jnp.zeros((d_model,), jnp.float32), 'Wk_r_w': w(ks[4], d_model, d_model), 'Wk_r_b': jnp.zeros((d_model,), jnp.float32), 'Wd_kv_w': w(ks[5], d_model, d_kv), 'Wd_kv_b': jnp.zeros((d_kv,), jnp.float32), 'Wu_k_w': w(ks[6], d_kv, d_model), 'Wu_k_b': jnp.zeros((d_model,), jnp.float32), 'Wu_v_w': w(ks[7], d_kv, d_model), 'Wu_v_b': jnp.zeros((d_model,), jnp.float32), 'Wo_w': w(ks[8], d_model, d_model), 'Wo_b': jnp.zeros((d_model,), jnp.float32)}
    _L0_attn_all = _L0_attn_setup()
    _L0_attn_in = {k: v for k, v in _L0_attn_all.items() if k in ('Wd_q_w', 'Wd_q_b', 'Wu_q_w', 'Wu_q_b', 'Wq_r_w', 'Wq_r_b', 'Wk_r_w', 'Wk_r_b', 'Wd_kv_w', 'Wd_kv_b', 'Wu_k_w', 'Wu_k_b', 'Wu_v_w', 'Wu_v_b', 'Wo_w', 'Wo_b')}
    del _L0_attn_all

    def _L0_ffn_setup():
        import jax, jax.numpy as jnp
        import numpy as np
        H = 512
        I = 512
        E = 8
        key = jax.random.key(seed)
        ks = jax.random.split(key, 8)
        s = 0.02
        x = jax.random.normal(ks[0], (4, 1024, H), dtype=jnp.float32)
        Wg = jax.random.normal(ks[1], (H, E), dtype=jnp.float32) * s
        bg = jnp.zeros((E,), dtype=jnp.float32)
        W1 = jax.random.normal(ks[2], (E, H, I), dtype=jnp.float32) * s
        b1 = jnp.zeros((E, I), dtype=jnp.float32)
        W2 = jax.random.normal(ks[3], (E, I, H), dtype=jnp.float32) * s
        b2 = jnp.zeros((E, H), dtype=jnp.float32)
        return {'x': x, 'Wg': Wg, 'bg': bg, 'W1': W1, 'b1': b1, 'W2': W2, 'b2': b2}
    _L0_ffn_all = _L0_ffn_setup()
    _L0_ffn_in = {k: v for k, v in _L0_ffn_all.items() if k in ('Wg', 'bg', 'W1', 'b1', 'W2', 'b2')}
    del _L0_ffn_all
    return {'x': x, 'ctx_1024': ctx_1024, 'L0_xattn_W_out': _L0_xattn_in['W_out'], 'L0_xattn_b_out': _L0_xattn_in['b_out'], 'L0_attn_Wd_q_w': _L0_attn_in['Wd_q_w'], 'L0_attn_Wd_q_b': _L0_attn_in['Wd_q_b'], 'L0_attn_Wu_q_w': _L0_attn_in['Wu_q_w'], 'L0_attn_Wu_q_b': _L0_attn_in['Wu_q_b'], 'L0_attn_Wq_r_w': _L0_attn_in['Wq_r_w'], 'L0_attn_Wq_r_b': _L0_attn_in['Wq_r_b'], 'L0_attn_Wk_r_w': _L0_attn_in['Wk_r_w'], 'L0_attn_Wk_r_b': _L0_attn_in['Wk_r_b'], 'L0_attn_Wd_kv_w': _L0_attn_in['Wd_kv_w'], 'L0_attn_Wd_kv_b': _L0_attn_in['Wd_kv_b'], 'L0_attn_Wu_k_w': _L0_attn_in['Wu_k_w'], 'L0_attn_Wu_k_b': _L0_attn_in['Wu_k_b'], 'L0_attn_Wu_v_w': _L0_attn_in['Wu_v_w'], 'L0_attn_Wu_v_b': _L0_attn_in['Wu_v_b'], 'L0_attn_Wo_w': _L0_attn_in['Wo_w'], 'L0_attn_Wo_b': _L0_attn_in['Wo_b'], 'L0_ffn_Wg': _L0_ffn_in['Wg'], 'L0_ffn_bg': _L0_ffn_in['bg'], 'L0_ffn_W1': _L0_ffn_in['W1'], 'L0_ffn_b1': _L0_ffn_in['b1'], 'L0_ffn_W2': _L0_ffn_in['W2'], 'L0_ffn_b2': _L0_ffn_in['b2']}

def reference(x, ctx_1024, L0_xattn_W_out, L0_xattn_b_out, L0_attn_Wd_q_w, L0_attn_Wd_q_b, L0_attn_Wu_q_w, L0_attn_Wu_q_b, L0_attn_Wq_r_w, L0_attn_Wq_r_b, L0_attn_Wk_r_w, L0_attn_Wk_r_b, L0_attn_Wd_kv_w, L0_attn_Wd_kv_b, L0_attn_Wu_k_w, L0_attn_Wu_k_b, L0_attn_Wu_v_w, L0_attn_Wu_v_b, L0_attn_Wo_w, L0_attn_Wo_b, L0_ffn_Wg, L0_ffn_bg, L0_ffn_W1, L0_ffn_b1, L0_ffn_W2, L0_ffn_b2):
    import jax
    import jax.numpy as jnp

    def _L0_xattn_ref(x, context, W_out, b_out, heads):
        import jax, jax.numpy as jnp
        import numpy as np
        b, i, dm = x.shape
        j = context.shape[1]
        d = dm // heads
        scale = d ** (-0.5)
        q = x.reshape(b, i, heads, d).transpose(0, 2, 1, 3)
        k = context.reshape(b, j, heads, d).transpose(0, 2, 1, 3)
        v = k
        sim = jnp.einsum('bhid,bhjd->bhij', q, k) * scale
        attn = jax.nn.softmax(sim, axis=-1)
        out = jnp.einsum('bhij,bhjd->bhid', attn, v)
        out = out.transpose(0, 2, 1, 3).reshape(b, i, dm)
        return out @ W_out.T + b_out

    def _L0_attn_ref(x, Wd_q_w, Wd_q_b, Wu_q_w, Wu_q_b, Wq_r_w, Wq_r_b, Wk_r_w, Wk_r_b, Wd_kv_w, Wd_kv_b, Wu_k_w, Wu_k_b, Wu_v_w, Wu_v_b, Wo_w, Wo_b):
        import jax, jax.numpy as jnp
        import numpy as np
        NUM_HEAD = 16
        D_Q = 256
        D_KV = 256
        ROPE_BASE = 10000.0

        def _cos_sin(seq_len, dim):
            pos = jnp.arange(seq_len, dtype=jnp.float32)[:, None]
            ids = jnp.arange(dim // 2, dtype=jnp.float32)
            theta = ROPE_BASE ** (-2.0 * ids) / (dim // 2)
            r = pos * theta[None, :]
            return (jnp.cos(r), jnp.sin(r))

        def _rope(x, cos, sin):
            b, s, d = x.shape
            xv = x.reshape(b, s, d // 2, 2)
            x0, x1 = (xv[..., 0], xv[..., 1])
            out = jnp.stack([x0 * cos - x1 * sin, x1 * cos + x0 * sin], axis=-1)
            return out.reshape(b, s, d)
        b, s, d_model = x.shape
        h = NUM_HEAD
        hd = d_model // h
        scale = jnp.sqrt(jnp.float32(h + D_KV + D_Q))

        def heads(t):
            return t.reshape(b, s, h, hd).transpose(0, 2, 1, 3)
        cos, sin = _cos_sin(s, d_model)
        ct_q = x @ Wd_q_w + Wd_q_b
        qt_c = heads(ct_q @ Wu_q_w + Wu_q_b)
        qt_r = heads(_rope(ct_q @ Wq_r_w + Wq_r_b, cos, sin))
        query = qt_c + qt_r
        ct_kv = x @ Wd_kv_w + Wd_kv_b
        kt_c = heads(ct_kv @ Wu_k_w + Wu_k_b)
        kt_r = heads(_rope(x @ Wk_r_w + Wk_r_b, cos, sin))
        key = kt_c + kt_r
        value = heads(ct_kv @ Wu_v_w + Wu_v_b)
        attn = jnp.einsum('bhqd,bhkd->bhqk', query, key) / scale
        attn = jax.nn.softmax(attn, axis=-1)
        out = jnp.einsum('bhqk,bhkd->bhqd', attn, value)
        out = out.transpose(0, 2, 1, 3).reshape(b, s, d_model)
        return out @ Wo_w + Wo_b

    def _L0_ffn_ref(x, Wg, bg, W1, b1, W2, b2):
        import jax, jax.numpy as jnp
        import numpy as np
        H = 512
        I = 512
        E = 8
        B, S, Hd = x.shape
        xf = x.reshape(-1, Hd)
        logits = xf @ Wg + bg
        gates = jax.nn.softmax(logits, axis=-1)
        idx = jnp.argmax(gates, axis=-1)
        h = jax.nn.gelu(jnp.einsum('th,ehi->tei', xf, W1) + b1, approximate=False)
        y = jnp.einsum('tei,eih->teh', h, W2) + b2
        out = jnp.take_along_axis(y, idx[:, None, None], axis=1)[:, 0, :]
        return out.reshape(B, S, Hd)
    x = x + _L0_xattn_ref(_layernorm(x, axis=-1), ctx_1024, L0_xattn_W_out, L0_xattn_b_out, 16)
    x = x + _L0_attn_ref(_layernorm(x, axis=-1), L0_attn_Wd_q_w, L0_attn_Wd_q_b, L0_attn_Wu_q_w, L0_attn_Wu_q_b, L0_attn_Wq_r_w, L0_attn_Wq_r_b, L0_attn_Wk_r_w, L0_attn_Wk_r_b, L0_attn_Wd_kv_w, L0_attn_Wd_kv_b, L0_attn_Wu_k_w, L0_attn_Wu_k_b, L0_attn_Wu_v_w, L0_attn_Wu_v_b, L0_attn_Wo_w, L0_attn_Wo_b)
    x = x + _L0_ffn_ref(_layernorm(x, axis=-1), L0_ffn_Wg, L0_ffn_bg, L0_ffn_W1, L0_ffn_b1, L0_ffn_W2, L0_ffn_b2)
    return x

_drawn_inputs = setup_inputs


def setup_inputs(seed=0):
    import zlib

    import numpy as np

    out = dict(_drawn_inputs(seed))
    spreads = {'L0_xattn_b_out': (0.0, 0.1),
     'L0_attn_Wd_q_b': (0.0, 0.8),
     'L0_attn_Wu_q_b': (0.0, 2.0),
     'L0_attn_Wq_r_b': (0.0, 2.0),
     'L0_attn_Wk_r_b': (0.0, 2.0),
     'L0_attn_Wd_kv_b': (0.0, 0.329),
     'L0_attn_Wu_k_b': (0.0, 2.0),
     'L0_attn_Wu_v_b': (0.0, 0.1),
     'L0_attn_Wo_b': (0.0, 0.1),
     'L0_ffn_bg': (0.0, 0.1),
     'L0_ffn_b1': (0.0, 0.348),
     'L0_ffn_b2': (0.0, 0.1)}
    factors = {'L0_attn_Wd_q_w': 8.0,
     'L0_attn_Wu_q_w': 8.0,
     'L0_attn_Wq_r_w': 8.0,
     'L0_attn_Wk_r_w': 8.0,
     'L0_attn_Wu_k_w': 8.0}
    for name, (base, spread) in spreads.items():
        noise = np.random.default_rng([zlib.crc32(name.encode()), seed]).standard_normal(out[name].shape)
        drawn = base * np.exp(spread * noise) if base else spread * noise
        out[name] = jnp.asarray(drawn.astype(out[name].dtype))
    for name, factor in factors.items():
        out[name] = (out[name] * factor).astype(out[name].dtype)
    return out
```

```python
from contextlib import ExitStack

import numpy as np
import concourse.bass as bass
from concourse import mybir

F32, F32R = mybir.dt.float32, mybir.dt.float32r
I32, U32 = mybir.dt.int32, mybir.dt.uint32
ALU, ACT, AX = mybir.AluOpType, mybir.ActivationFunctionType, mybir.AxisListType

P = 128
B, S, D = 64, 32, 512
J = 257
H, HD = 16, 32
G, HL = D // P, P // HD
BT = P // S
T = B * S // P
C2 = (J - 1) // P
DQ = 256
E, FI = 8, 512
SLOTS = T + E - 1
SW = 24
BIG = 4096
EPS = 1e-5
XSCALE = float(HD) ** -0.5
SSCALE = float(1.0 / np.sqrt(np.float32(H + DQ + DQ)))


def constant_table():
    p = np.arange(P)
    pos = (p % S).astype(np.float32)[:, None]
    ids = np.arange(D // 2, dtype=np.float32)
    theta = np.power(np.float32(10000.0), np.float32(-2.0) * ids) / np.float32(D // 2)
    angle = (pos * theta[None, :]).astype(np.float32)
    cos, sin = np.cos(angle).astype(np.float32), np.sin(angle).astype(np.float32)
    parts = {
        "ident": np.eye(P),
        "samehead": (p[:, None] // HD == p[None, :] // HD),
        "latent": (p[:, None] % S == np.arange(S)[None, :]),
        "before": (p[:, None] < p[None, :]),
        "ones": np.ones((P, P)),
        "cos": np.repeat(cos, 2, axis=1),
        "sin": np.stack([-sin, sin], axis=-1).reshape(P, D),
        "iota": np.tile(np.arange(P), (P, 1)),
        "token": p[:, None] + P * np.arange(T)[None, :] - BIG,
        "row": np.repeat(p[:, None], SW, axis=1),
        "minushalf": np.full((P, 1), -0.5),
    }
    at, start = {}, 0
    for name, a in parts.items():
        at[name] = (start, start + a.shape[1])
        start += a.shape[1]
    return np.concatenate([a.astype(np.float32) for a in parts.values()], axis=1), at


class Signal:

    def __init__(self, handle):
        self.handle, self.count = handle, 0


class Queue:

    def __init__(self, engine):
        self.engine, self.passed = engine, {}

    def wait(self, *points):
        for signal, value in points:
            if self.passed.get(signal, 0) < value:
                self.passed[signal] = value
                self.engine.wait_ge(signal.handle, value)

    def do(self, make, signal, by=1):
        make(self.engine).then_inc(signal.handle, by)
        signal.count += by
        return signal, signal.count


class Buffer:

    def __init__(self, tensor):
        self.t, self.free = tensor, []


def program(nc, ins, out, const_at, x2_dram, v_dram):
    ctx = ExitStack()
    names = {}

    def uniq(name):
        names[name] = names.get(name, 0) + 1
        return name if names[name] == 1 else f"{name}_{names[name]}"

    def signal(name):
        return Signal(ctx.enter_context(nc.semaphore(uniq(name))))

    def sb(name, shape, dt=F32, stack=ctx):
        return stack.enter_context(nc.sbuf_tensor(uniq(name), shape, dt))

    pe, act, dve, pool, sp = (Queue(e) for e in (nc.tensor, nc.scalar, nc.vector, nc.gpsimd, nc.sync))
    done = {q: signal(n) for q, n in ((pe, "pe_done"), (act, "act_done"), (dve, "dve_done"), (pool, "pool_done"))}

    def on(queue, make, *waits):
        queue.wait(*waits)
        return queue.do(make, done[queue])

    consts = sb("consts", [P, const_at["minushalf"][1]])

    def const(name):
        a, b = const_at[name]
        return consts[:, a:b]

    ident, samehead, latent = const("ident"), const("samehead"), const("latent")
    cos, sin = const("cos"), const("sin")
    last_t = sb("last_t", [P, G, B])
    running = sb("running", [P, E])
    onehot = sb("onehot", [P, T, E])
    rank = sb("rank", [P, T])
    phase = ExitStack()

    def sba(name, shape, dt=F32):
        return sb(name, shape, dt, phase)

    bias = {n: sba(f"bias_{n}", [P, D]) for n in ("xout", "ct", "q", "k", "v", "out")}
    bias_g = sba("bias_g", [P, E])
    wg = sba("wg", [P, G, E])
    weight = {n: (sba(f"{n}_hi", [P, k, D], F32R), sba(f"{n}_lo", [P, k, D], F32R))
              for n, k in (("xout", 4), ("ct", 4), ("qr", 2), ("qc", 2), ("kr", 4), ("kc", 2), ("v", 2), ("out", 4))}

    x_tile = [Buffer(sba(f"x{i}", [P, D])) for i in range(3)]
    context = [Buffer(sba(f"context{i}", [P, C2, D])) for i in range(3)]
    k_t = [Buffer(sba(f"k_t{i}", [P, G, J + 1])) for i in range(2)]
    prob = [Buffer(sba(f"prob{i}", [P, G, J])) for i in range(2)]
    prob_t = [Buffer(sba(f"prob_t{i}", [P, G, C2, P])) for i in range(2)]
    qblock = Buffer(sba("qblock", [P, BT, G, HL, S]))
    qblock2 = Buffer(sba("qblock2", [P, BT, G, HL, S]))
    vblock = Buffer(sba("vblock", [P, G, BT, HL, HD]))
    negmax = [Buffer(sba(f"negmax{i}", [P, G])) for i in range(2)]
    sums = [Buffer(sba(f"sums{i}", [P, G, BT])) for i in range(2)]
    plast = [Buffer(sba(f"plast{i}", [P, G, BT])) for i in range(2)]
    rsum = Buffer(sba("rsum", [P, G, BT]))
    att_raw = Buffer(sba("att_raw", [P, G, BT, S]))
    lhs = [(Buffer(sba(f"lhs_hi{i}", [P, G, P], F32R)), Buffer(sba(f"lhs_lo{i}", [P, G, P], F32R))) for i in range(2)]
    norm_x, norm_s = Buffer(sba("norm_x", [P, D])), Buffer(sba("norm_s", [P, D]))
    work = [Buffer(sba(f"work{i}", [P, D])) for i in range(5)]
    small = {}
    for n, w in (("stats", 6), ("mean_var", 2), ("var_eps", 1), ("rstd", 1)):
        for who in ("x", "s"):
            small[n, who] = sba(f"{n}_{who}", [P, w])
    smax, ssum = sba("smax", [P, G, BT]), sba("ssum", [P, G, BT])
    logits, top = sba("logits", [P, E]), sba("top", [P, 8])
    top_at, expert = sba("top_at", [P, 8], U32), sba("expert", [P, 1])
    place = sba("place", [P, E])

    psum = [Buffer(ctx.enter_context(nc.psum_tensor(f"bank{i}", [P, 512], F32))) for i in range(8)]
    score_banks, turn_banks, att_bank, self_banks = psum[0:2], psum[2:4], psum[4], psum[5:8]
    taken = {"turn": 0, "self": 0, "lhs": 0, "work": 0}

    def ring(name, buffers):
        taken[name] += 1
        return buffers[(taken[name] - 1) % len(buffers)]

    s_const = signal("const_loaded")
    const_in = sp.do(lambda e: e.dma_start(consts[:, :], ins["const"]), s_const, 16)
    s_x = [signal(f"x_loaded{i}") for i in range(len(x_tile))]
    s_context = [signal(f"context_loaded{i}") for i in range(len(context))]
    x_rows = ins["x"].rearrange("b s d -> (b s) d").rearrange("(t p) d -> t p d", p=P)
    x_in, context_in = {}, {}

    def load_x(t):
        buf = x_tile[t % len(x_tile)]
        sp.wait(*buf.free)
        x_in[t] = sp.do(lambda e: e.dma_start(buf.t[:, :], x_rows[t]), s_x[t % len(x_tile)], 16)

    def load_context(b):
        buf = context[b % len(context)]
        sp.wait(*buf.free)
        src = ins["ctx_1024"][b, 0:C2 * P, :].rearrange("(p c) d -> p c d", c=C2)
        context_in[b] = sp.do(lambda e: e.dma_start(buf.t[:, :, :], src), s_context[b % len(context)], 16)

    zeroed = [on(pool, lambda e, z=z: e.memset(z.t[:, :, :, :, :], 0.0)) for z in (qblock,)]
    zeroed_running = on(pool, lambda e: e.memset(running[:, :], 0.0))
    load_x(0)
    load_context(0)
    load_context(1)
    s_last = signal("last_rows_loaded")
    last_in = sp.do(lambda e: e.dma_start(norm_s.t[0:B, :], ins["ctx_1024"][:, J - 1, :]), s_last, 16)
    load_context(2)

    def set_up():
        bank = ring("self", self_banks)
        pe.wait(last_in, const_in)
        for g in range(G):
            point = on(pe, lambda e, g=g: e.transpose(bank.t[:, g * B:(g + 1) * B], norm_s.t[0:B, g * P:(g + 1) * P],
                                                      ident[0:B, 0:B]))
        norm_s.free = [point]
        ready["last_t"] = on(act, lambda e: e.activation(last_t[:, :, :].rearrange("p g b -> p (g b)"),
                                                         bank.t[:, 0:G * B], ACT.Copy), point)
        bank.free = [ready["last_t"]]
        yield
        def bcast(dst, src, name):
            s = signal(f"bias_{name}_loaded")
            n = src.shape[0]
            return act.do(lambda e: e.dma_start(dst, src.unsqueeze(0).broadcast_to([P, n])), s, 16)

        ready["bias_xout"] = bcast(bias["xout"][:, :], ins["L0_xattn_b_out"], "xout")
        ready["bias_ct0"] = bcast(bias["ct"][:, 0:DQ], ins["L0_attn_Wd_q_b"], "ct_q")
        ready["bias_ct1"] = bcast(bias["ct"][:, DQ:D], ins["L0_attn_Wd_kv_b"], "ct_kv")
        ready["bias_v"] = bcast(bias["v"][:, :], ins["L0_attn_Wu_v_b"], "v")
        ready["bias_out"] = bcast(bias["out"][:, :], ins["L0_attn_Wo_b"], "out")
        ready["bias_g"] = bcast(bias_g[:, :], ins["L0_ffn_bg"], "gate")
        s_wg = signal("wg_loaded")
        ready["wg"] = act.do(lambda e: e.dma_start(wg[:, :, :], ins["L0_ffn_Wg"].rearrange("(g p) e -> p g e", p=P)), s_wg, 16)
        yield
        for n, plain, rot in (("q", "L0_attn_Wu_q_b", "L0_attn_Wq_r_b"), ("k", "L0_attn_Wu_k_b", "L0_attn_Wk_r_b")):
            rot_b, turned, plain_b = work[0], work[1], work[2]
            act.wait(*rot_b.free, *plain_b.free)
            rot_in = bcast(rot_b.t[:, :], ins[rot], f"{n}_rot")
            plain_in = bcast(plain_b.t[:, :], ins[plain], f"{n}_plain")
            dve.wait(const_in)
            a = on(dve, lambda e: e.tensor_tensor(bias[n][:, :], rot_b.t[:, :], cos, ALU.mult), rot_in)
            for o in range(2):
                b = on(dve, lambda e, o=o: e.tensor_tensor(halves(turned.t)[:, :, o], halves(rot_b.t)[:, :, 1 - o],
                                                           sin.rearrange("p (i o) -> p i o", o=2)[:, :, o], ALU.mult))
            c = on(dve, lambda e: e.tensor_tensor(bias[n][:, :], bias[n][:, :], turned.t[:, :], ALU.add), a, b)
            d = on(dve, lambda e: e.tensor_tensor(bias[n][:, :], bias[n][:, :], plain_b.t[:, :], ALU.add), c, plain_in)
            rot_b.free, plain_b.free = [b], [d]
            ready[f"bias_{n}"] = d
            yield
        staging = [(qblock2, signal("weight_loaded0")), (vblock, signal("weight_loaded1"))]
        flat = {id(z): z.t[:, :, :, :, :].rearrange("p a b c d -> p (a b c d)").rearrange("p (k n) -> p k n", k=4)
                for z, _ in staging}
        plan = [("xout", [("L0_xattn_W_out", 0)]), ("ct", [("L0_attn_Wd_q_w", 0), ("L0_attn_Wd_kv_w", DQ)]),
                ("qr", [("L0_attn_Wq_r_w", 0)]), ("qc", [("L0_attn_Wu_q_w", 0)]), ("kr", [("L0_attn_Wk_r_w", 0)]),
                ("kc", [("L0_attn_Wu_k_w", 0)]), ("v", [("L0_attn_Wu_v_w", 0)]), ("out", [("L0_attn_Wo_w", 0)])]
        for i, (n, sources) in enumerate(plan):
            buf, s_in = staging[i % 2]
            stage = flat[id(buf)]
            sp.wait(*buf.free)
            for name, col in sources:
                w = ins[name]
                k, width = w.shape[0] // P, w.shape[1]
                point = sp.do(lambda e, w=w, col=col, k=k, width=width, stage=stage:
                              e.dma_start(stage[:, 0:k, col:col + width], w.rearrange("(k p) n -> p k n", p=P)), s_in, 16)
            hi, lo = weight[n]
            if n == "xout":
                for c in range(G):
                    bank = ring("self", self_banks)
                    pe.wait(point, *bank.free)
                    for o in range(G):
                        turned = on(pe, lambda e, o=o, c=c, bank=bank, stage=stage: e.transpose(
                            bank.t[:, o * P:(o + 1) * P], stage[:, o, c * P:(c + 1) * P], ident))
                    a = on(act, lambda e, c=c, bank=bank: e.activation(hi[:, c, :], bank.t[:, :], ACT.Copy), turned)
                    b = on(dve, lambda e, c=c, bank=bank: e.tensor_tensor(
                        lo[:, c, :], bank.t[:, :], hi[:, c, :].bitcast(F32), ALU.subtract), a)
                    bank.free = [b]
                    yield
                buf.free = [turned]
            else:
                for c in range(k):
                    a = on(act, lambda e, c=c, stage=stage, hi=hi: e.activation(hi[:, c, :], stage[:, c, :], ACT.Copy), point)
                    b = on(dve, lambda e, c=c, stage=stage, hi=hi, lo=lo: e.tensor_tensor(
                        lo[:, c, :], stage[:, c, :], hi[:, c, :].bitcast(F32), ALU.subtract), a)
                    yield
                buf.free = [b]
            ready[f"w_{n}"] = b
        for z, _ in staging:
            zeroed.append(on(pool, lambda e, z=z: e.memset(z.t[:, :, :, :, :], 0.0), *z.free))
            z.free = [zeroed[-1]]
        yield

    ready = {}

    def halves(t):
        return t[:, :].rearrange("p (i o) -> p i o", o=2)

    def layer_norm(x, x_ready, dst, who):
        stats, mv, ve, rstd = (small[n, who] for n in ("stats", "mean_var", "var_eps", "rstd"))
        a = on(dve, lambda e: e.bn_stats(stats[:, :], x), x_ready)
        a = on(dve, lambda e: e.bn_aggr(mv[:, :], stats[:, :]), a)
        b = on(pool, lambda e: e.tensor_scalar(ve[:, :], mv[:, 1:2], EPS, None, ALU.add), a)
        c = on(pool, lambda e: e.tensor_tensor(rstd[:, :], ve[:, :], const("minushalf"), ALU.pow), b, const_in)
        return on(dve, lambda e: e.tensor_scalar(dst.t[:, :], x, mv[:, 0:1], rstd[:, :], ALU.subtract, ALU.mult),
                  c, *dst.free)

    def turn(src, src_ready, bank, stride=1):
        pe.wait(src_ready, const_in, *bank.free)
        for g in range(G):
            part = src[:, g * P:(g + 1) * P] if stride == 1 else src[:, g::stride]
            point = on(pe, lambda e, g=g, part=part: e.transpose(bank.t[:, g * P:(g + 1) * P], part, ident))
        return point

    def split(src, src_ready, release):
        hi, lo = ring("lhs", lhs)
        flat = src.rearrange("p (g n) -> p g n", g=G) if len(src.shape) == 2 else src
        a = on(act, lambda e: e.activation(hi.t[:, :, :], flat, ACT.Copy), src_ready, *hi.free)
        b = on(dve, lambda e: e.tensor_tensor(lo.t[:, :, :], flat, hi.t[:, :, :].bitcast(F32), ALU.subtract), a, *lo.free)
        release.free = [b]
        return hi, lo, b

    def dense(operand, chunks, name, bank):
        hi, lo, point = operand
        w_hi, w_lo = weight[name]
        pe.wait(point, ready[f"w_{name}"], *bank.free)
        n = len(chunks)
        for i, c in enumerate(chunks):
            for j, (l, r) in enumerate(((hi, w_hi), (hi, w_lo), (lo, w_hi))):
                point = on(pe, lambda e, i=i, c=c, l=l, r=r, j=j: e.matmul(
                    bank.t[:, :], l.t[:, c, :], r[:, i, :], start=(i == 0 and j == 0), stop=(i == n - 1 and j == 2)))
        hi.free, lo.free = [point], [point]
        return point

    def block_diagonal(bank, turned, dst, scale):
        src = bank.t[:, :].rearrange("p (g b i) -> p b g i", g=G, b=BT)
        points = []
        for hl in range(HL):
            rows = slice(hl * HD, (hl + 1) * HD)
            if hl < HL // 2:
                points.append(on(act, lambda e, rows=rows, hl=hl: e.activation(
                    dst.t[rows, :, :, hl, :], src[rows], ACT.Copy, scale=scale), turned, *dst.free))
            else:
                points.append(on(dve, lambda e, rows=rows, hl=hl: e.tensor_scalar(
                    dst.t[rows, :, :, hl, :], src[rows], scale, None, ALU.mult), turned, *dst.free))
        last = [points[HL // 2 - 1], points[-1]]
        bank.free = last
        return last

    scored, turned_p, context_used, q_ready = {}, {}, {}, {}

    def queries(t):
        xb = x_tile[t % len(x_tile)]
        point = layer_norm(xb.t[:, :], x_in[t], norm_x, "x")
        bank = ring("turn", turn_banks)
        turned = turn(norm_x.t, point, bank)
        norm_x.free = [turned]
        return bank, turned

    def place_queries(t, bank, turned):
        pool_zero = zeroed[0]
        act.wait(pool_zero)
        dve.wait(pool_zero)
        q_ready[t] = block_diagonal(bank, turned, qblock, XSCALE)

    k_ready = {}

    def turn_context(b, pair):
        buf, kb = context[b % len(context)], k_t[b % 2]
        bank = ring("turn", turn_banks)
        pe.wait(context_in[b], const_in, *bank.free)
        for gg in range(2):
            for c in range(C2):
                g = 2 * pair + gg
                point = on(pe, lambda e, g=g, gg=gg, c=c: e.transpose(
                    bank.t[:, (gg * C2 + c) * P:(gg * C2 + c + 1) * P], buf.t[:, c, g * P:(g + 1) * P], ident))
        dst = kb.t[:, 2 * pair:2 * pair + 2, 0:C2 * P]
        src = bank.t[:, :].rearrange("p (g n) -> p g n", g=2)
        if pair == 0:
            moved = on(act, lambda e: e.activation(dst, src, ACT.Copy), point, *kb.free)
            last = on(pool, lambda e: e.tensor_copy(kb.t[:, :, J - 1:J].rearrange("p g o -> p (g o)"), last_t[:, :, b]),
                      ready["last_t"], *kb.free)
            k_ready[b] = [moved, last]
        else:
            moved = on(dve, lambda e: e.tensor_copy(dst, src), point, *kb.free)
            k_ready[b].append(moved)
        bank.free = [moved]

    def score(b, g):
        t, bl = divmod(b, BT)
        bank, pb, nm, sm = score_banks[g % 2], prob[b % 2], negmax[b % 2], sums[t % 2]
        need = k_ready[b] if g >= 2 else k_ready[b][0:2]
        pe.wait(*q_ready[t], *need, *bank.free)
        point = on(pe, lambda e: e.matmul(bank.t[:, 0:J], qblock.t[:, bl, g, :, :], k_t[b % 2].t[:, g, 0:J],
                                          start=True, stop=True))
        if g == G - 1:
            k_t[b % 2].free = [point]
            if bl == BT - 1:
                qblock.free = [point]
        largest = on(dve, lambda e: e.tensor_reduce(nm.t[:, g:g + 1], bank.t[:, 0:J], AX.X, ALU.max, negate=True),
                     point, *nm.free)
        scored[b, g] = on(act, lambda e: e.activation(pb.t[:, g, :], bank.t[:, 0:J], ACT.Exp, bias=nm.t[:, g:g + 1],
                                                      accum_out=sm.t[:, g, bl:bl + 1]),
                          largest, *pb.free, *sm.free)
        bank.free = [scored[b, g]]
        if g == G - 1:
            nm.free = [scored[b, g]]
            kept = on(pool, lambda e: e.tensor_copy(plast[t % 2].t[:, :, bl], pb.t[:, :, J - 1:J].rearrange("p g o -> p (g o)")),
                      scored[b, g], *plast[t % 2].free)
            scored[b, "last"] = kept

    p_ready = {}

    def turn_prob(b, pair):
        pb, tb = prob[b % 2], prob_t[b % 2]
        bank = ring("turn", turn_banks)
        pe.wait(scored[b, 2 * pair + 1], *bank.free)
        for gg in range(2):
            for c in range(C2):
                g = 2 * pair + gg
                point = on(pe, lambda e, g=g, gg=gg, c=c: e.transpose(
                    bank.t[:, (gg * C2 + c) * P:(gg * C2 + c + 1) * P], pb.t[:, g, c * P:(c + 1) * P], ident))
        dst = tb.t[:, 2 * pair:2 * pair + 2, :, :].rearrange("p g c n -> p (g c n)")
        if pair == 0:
            moved = on(dve, lambda e: e.tensor_copy(dst, bank.t[:, :]), point, *tb.free)
        else:
            moved = on(act, lambda e: e.activation(dst, bank.t[:, :], ACT.Copy), point, *tb.free)
            pb.free = [point, scored[b, "last"]]
        p_ready[b, pair] = moved
        bank.free = [moved]

    raw_ready = {}

    def attend(b, pair):
        t, bl = divmod(b, BT)
        cb, tb, raw = context[b % len(context)], prob_t[b % 2], att_raw
        pe.wait(p_ready[b, pair], context_in[b])
        if pair == 0:
            pe.wait(*att_bank.free)
        for g in (2 * pair, 2 * pair + 1):
            for c in range(C2):
                point = on(pe, lambda e, g=g, c=c: e.matmul(
                    att_bank.t[:, g * P:(g + 1) * P], cb.t[:, c, g * P:(g + 1) * P], tb.t[:, g, c, :],
                    start=(c == 0), stop=(c == C2 - 1)))
        if pair == 1:
            cb.free, tb.free = [point], [point]
            src = att_bank.t[:, :].rearrange("p (g h i) -> p g h i", g=G, h=HL)
            points = []
            for hl in range(HL):
                rows = slice(hl * HD, (hl + 1) * HD)
                if hl % 2:
                    points.append(on(act, lambda e, rows=rows, hl=hl: e.activation(
                        raw.t[rows, :, bl, :], src[rows, :, hl, :], ACT.Copy), point, *raw.free))
                else:
                    points.append(on(dve, lambda e, rows=rows, hl=hl: e.tensor_copy(
                        raw.t[rows, :, bl, :], src[rows, :, hl, :]), point, *raw.free))
            att_bank.free = points[2:]
            raw_ready[b] = points[2:]
            if b + len(context) < B:
                load_context(b + len(context))

    def cross_stream():
        bank, turned = queries(0)
        place_queries(0, bank, turned)
        for pair in range(2):
            turn_context(0, pair)
        yield -1
        for b in range(B):
            t, bl = divmod(b, BT)
            score(b, 0)
            yield b
            score(b, 1)
            yield b
            if b:
                attend(b - 1, 1)
                if bl == 0:
                    finished.append(t - 1)
                yield b
            if b + 1 < B:
                turn_context(b + 1, 0)
                yield b
            score(b, 2)
            yield b
            turn_prob(b, 0)
            yield b
            score(b, 3)
            if bl == 1 and t + 1 < T:
                assert t < 2 or routed[-1] == t - 2
                load_x(t + 1)
            yield b
            if b + 1 < B:
                turn_context(b + 1, 1)
                yield b
            attend(b, 0)
            if bl == BT - 1 and t + 1 < T:
                bank, turned = queries(t + 1)
                yield b
                place_queries(t + 1, bank, turned)
            yield b
            turn_prob(b, 1)
            yield b
        attend(B - 1, 1)
        finished.append(T - 1)

    finished = []

    s_v_out = [signal(f"v_stored{i}") for i in range(2)]
    s_v_in = [signal(f"v_spread{i}") for i in range(HL)]
    v_dram_free = [[], []]
    s_x2 = [signal(f"x2_stored{i}") for i in range(len(x_tile))]
    x2_out = {}

    def rotate(name, operand, chunks, plain_operand, plain_chunks):
        kind = name
        bank = ring("self", self_banks)
        point = dense(operand, chunks, f"{kind}r", bank)
        kept, turned = ring("work", work), ring("work", work)
        a = on(dve, lambda e: e.tensor_tensor(kept.t[:, :], bank.t[:, :], cos, ALU.mult), point, *kept.free)
        dve.wait(*turned.free)
        src = bank.t[:, :].rearrange("p (i o) -> p i o", o=2)
        sin2 = sin.rearrange("p (i o) -> p i o", o=2)
        for o in range(2):
            b = on(dve, lambda e, o=o: e.tensor_tensor(halves(turned.t)[:, :, o], src[:, :, 1 - o], sin2[:, :, o], ALU.mult))
        bank.free = [b]
        b = on(pool, lambda e: e.tensor_tensor(turned.t[:, :], turned.t[:, :], bias[kind][:, :], ALU.add), b, ready[f"bias_{kind}"])
        yield
        bank = ring("self", self_banks)
        point = dense(plain_operand, plain_chunks, f"{kind}c", bank)
        a = on(dve, lambda e: e.tensor_tensor(kept.t[:, :], kept.t[:, :], bank.t[:, :], ALU.add), point, a)
        bank.free = [a]
        a = on(pool, lambda e: e.tensor_tensor(kept.t[:, :], kept.t[:, :], turned.t[:, :], ALU.add), a, b)
        turned.free = [a]
        results[kind] = (kept, a)
        yield

    results = {}

    def self_tile(t):
        k = t % 2
        xb = x_tile[t % len(x_tile)]
        raw, sm, pl = att_raw, sums[k], plast[k]
        exps = [scored[b, G - 1] for b in range(BT * t, BT * t + BT)]
        x_plus = on(pool, lambda e: e.tensor_tensor(xb.t[:, :], xb.t[:, :], bias["xout"][:, :], ALU.add),
                    ready["bias_xout"], *q_ready[t])
        inv = on(dve, lambda e: e.reciprocal(rsum.t[:, :, :], sm.t[:, :, :]), exps[-1], *rsum.free)
        sm.free = [inv]
        shape4 = lambda t_: t_[:, :].rearrange("p (g b i) -> p g b i", g=G, b=BT)
        lat = latent.unsqueeze(1).unsqueeze(1).broadcast_to([P, G, BT, S])
        spread_by = []
        spread = [ring("work", work) for _ in range(2)]
        for i, (src, src_ready) in enumerate(((pl, scored[BT * t + BT - 1, "last"]), (rsum, inv))):
            per_head = src.t[:, :, :].unsqueeze(3).broadcast_to([P, G, BT, S])
            point = on(pool, lambda e, i=i, per_head=per_head: e.tensor_tensor(shape4(spread[i].t), per_head, lat, ALU.mult),
                       src_ready, const_in, *spread[i].free)
            src.free = [point]
            spread_by.append(point)
        yield
        yield
        spread_banks = []
        for i in range(2):
            bank = ring("self", self_banks)
            point = on(pe, lambda e, i=i, bank=bank: e.matmul(
                bank.t[:, :], samehead, spread[i].t[:, :], start=True, stop=True),
                spread_by[i], *bank.free)
            spread[i].free = [point]
            spread_banks.append((bank, point))
        att = ring("work", work)
        (bank, point), (bank_inv, point_inv) = spread_banks
        last = last_t[:, :, BT * t:BT * t + BT].unsqueeze(3).broadcast_to([P, G, BT, S])
        a = on(dve, lambda e: e.tensor_tensor(shape4(att.t), shape4(bank.t), last, ALU.mult), point, ready["last_t"], *att.free)
        bank.free = [a]
        a = on(dve, lambda e: e.tensor_tensor(shape4(att.t), shape4(att.t), raw.t[:, :, :, :], ALU.add), a,
               *[p for b in range(BT * t, BT * t + BT) for p in raw_ready[b]])
        raw.free = [a]
        a = on(dve, lambda e: e.tensor_tensor(att.t[:, :], att.t[:, :], bank_inv.t[:, :], ALU.mult), a, point_inv)
        bank_inv.free = [a]
        operand = split(att.t[:, :], a, att)
        yield
        yield
        bank = ring("self", self_banks)
        point = dense(operand, range(G), "xout", bank)
        x1 = on(dve, lambda e: e.tensor_tensor(xb.t[:, :], xb.t[:, :], bank.t[:, :], ALU.add), point, x_plus)
        bank.free = [x1]
        yield
        point = layer_norm(xb.t[:, :], x1, norm_s, "s")
        x_plus = on(pool, lambda e: e.tensor_tensor(xb.t[:, :], xb.t[:, :], bias["out"][:, :], ALU.add), point, ready["bias_out"])
        yield
        yield
        bank = ring("self", self_banks)
        turned = turn(norm_s.t, point, bank)
        norm_s.free = [turned]
        normed = split(bank.t[:, :], turned, bank)
        yield
        yield
        bank = ring("self", self_banks)
        point = dense(normed, range(G), "ct", bank)
        low = ring("work", work)
        low_ready = on(dve, lambda e: e.tensor_tensor(low.t[:, :], bank.t[:, :], bias["ct"][:, :], ALU.add),
                       point, ready["bias_ct0"], ready["bias_ct1"], *low.free)
        bank.free = [low_ready]
        yield
        bank = ring("self", self_banks)
        turned = turn(low.t, low_ready, bank)
        low.free = [turned]
        low_t = split(bank.t[:, :], turned, bank)
        yield
        q_part, kv_part = range(0, 2), range(2, 4)
        yield from rotate("k", normed, range(G), low_t, kv_part)
        k_buf, k_point = results["k"]
        yield from rotate("q", low_t, q_part, low_t, q_part)
        q_buf, q_point = results["q"]
        bank = ring("self", self_banks)
        turned = turn(k_buf.t, k_point, bank)
        k_buf.free = [turned]
        k2_t = ring("work", work)
        k2 = on(act, lambda e: e.activation(k2_t.t[:, :], bank.t[:, :], ACT.Copy),
                turned, *k2_t.free)
        bank.free = [k2]
        yield
        bank = ring("self", self_banks)
        point = dense(low_t, kv_part, "v", bank)
        v_buf = ring("work", work)
        v_point = on(dve, lambda e: e.tensor_tensor(v_buf.t[:, :], bank.t[:, :], bias["v"][:, :], ALU.add),
                     point, ready["bias_v"], *v_buf.free)
        bank.free = [v_point]
        sp.wait(v_point, *v_dram_free[k])
        stored = sp.do(lambda e: e.dma_start(v_dram[k], v_buf.t[:, :]), s_v_out[k], 16)
        v_buf.free = [stored]
        sp.wait(stored, *vblock.free)
        v_in = []
        for hl in range(HL):
            for g in range(G):
                src = v_dram[k].rearrange("(b j) (g h d) -> h g j b d", b=BT, g=G, h=HL)[hl, g]
                point = sp.do(lambda e, hl=hl, g=g, src=src: e.dma_start(
                    vblock.t[hl * S:(hl + 1) * S, g, :, hl, :], src), s_v_in[hl], 16)
            v_in.append(point)
        v_dram_free[k] = v_in
        yield
        bank = ring("self", self_banks)
        turned = turn(q_buf.t, q_point, bank)
        q_buf.free = [turned]
        q2 = block_diagonal(bank, turned, qblock2, SSCALE)
        yield
        yield
        bank = ring("self", self_banks)
        pe.wait(*q2, k2, *bank.free)
        for g in range(G):
            for bl in range(BT):
                at = (g * BT + bl) * S
                point = on(pe, lambda e, g=g, bl=bl, at=at: e.matmul(
                    bank.t[:, at:at + S], qblock2.t[:, bl, g, :, :], k2_t.t[:, g * P + bl * S:g * P + (bl + 1) * S], start=True, stop=True))
        qblock2.free, k2_t.free = [point], [point]
        grid = lambda t_: t_[:, :].rearrange("p (n j) -> p n j", j=S)
        per = lambda s_: s_[:, :, :].rearrange("p g b -> p (g b)").unsqueeze(2).broadcast_to([P, G * BT, S])
        flat16 = lambda s_: s_[:, :, :].rearrange("p g b -> p (g b)")
        soft, soft_t = ring("work", work), ring("work", work)
        a = on(dve, lambda e: e.tensor_reduce(flat16(smax), grid(bank.t), AX.X, ALU.max), point)
        a = on(dve, lambda e: e.tensor_tensor(grid(soft.t), grid(bank.t), per(smax), ALU.subtract), a, *soft.free)
        bank.free = [a]
        a = on(act, lambda e: e.activation(soft.t[:, :], soft.t[:, :], ACT.Exp), a)
        yield
        b = on(dve, lambda e: e.tensor_reduce(flat16(ssum), grid(soft.t), AX.X, ALU.add), a)
        b = on(dve, lambda e: e.reciprocal(ssum[:, :, :], ssum[:, :, :]), b)
        a = on(pool, lambda e: e.tensor_tensor(grid(soft.t), grid(soft.t), per(ssum), ALU.mult), b)
        soft_point = on(dve, lambda e: e.transpose(soft_t.t[:, :], soft.t[:, :]), a, *soft_t.free)
        soft.free = [soft_point]
        yield
        yield
        bank = ring("self", self_banks)
        pe.wait(soft_point, *v_in, *bank.free)
        for g in range(G):
            for bl in range(BT):
                at = (g * BT + bl) * S
                point = on(pe, lambda e, g=g, bl=bl, at=at: e.matmul(
                    bank.t[:, at:at + S], vblock.t[:, g, bl, :, :], soft_t.t[:, at:at + S], start=True, stop=True))
        vblock.free, soft_t.free = [point], [point]
        operand = split(bank.t[:, :], point, bank)
        yield
        yield
        bank = ring("self", self_banks)
        point = dense(operand, range(G), "out", bank)
        x2 = on(dve, lambda e: e.tensor_tensor(xb.t[:, :], xb.t[:, :], bank.t[:, :], ALU.add), point, x_plus)
        bank.free = [x2]
        sp.wait(x2)
        x2_out[t] = sp.do(lambda e: e.dma_start(x2_dram[t * P:(t + 1) * P, :], xb.t[:, :]), s_x2[t % len(x_tile)], 16)
        yield
        point = layer_norm(xb.t[:, :], x2, norm_s, "s")
        xb.free = [x2_out[t], point]
        yield
        yield
        bank = ring("self", self_banks)
        turned = turn(norm_s.t, point, bank)
        norm_s.free = [turned]
        x3 = ring("work", work)
        x3_point = on(act, lambda e: e.activation(x3.t[:, :], bank.t[:, :], ACT.Copy), turned, *x3.free)
        bank.free = [x3_point]
        yield
        bank = ring("self", self_banks)
        pe.wait(x3_point, ready["wg"], *bank.free)
        for g in range(G):
            point = on(pe, lambda e, g=g: e.matmul(bank.t[:, 0:E], x3.t[:, g * P:(g + 1) * P], wg[:, g, :],
                                                   start=(g == 0), stop=(g == G - 1)))
        x3.free = [point]
        a = on(dve, lambda e: e.tensor_tensor(logits[:, :], bank.t[:, 0:E], bias_g[:, :], ALU.add), point, ready["bias_g"])
        bank.free = [a]
        a = on(dve, lambda e: e.max(top[:, :], logits[:, :]), a)
        a = on(dve, lambda e: e.max_index(top_at[:, :], top[:, :], logits[:, :]), a)
        a = on(dve, lambda e: e.tensor_copy(expert[:, :], top_at[:, 0:1]), a)
        hot = on(dve, lambda e: e.tensor_scalar(onehot[:, t, :], const("iota")[:, 0:E], expert[:, :], None, ALU.is_equal), a)
        yield
        yield
        bank = ring("self", self_banks)
        pe.wait(hot, *bank.free)
        on(pe, lambda e: e.matmul(bank.t[:, 0:E], const("before"), onehot[:, t, :], start=True, stop=True))
        point = on(pe, lambda e: e.matmul(bank.t[:, E:2 * E], const("ones"), onehot[:, t, :], start=True, stop=True))
        a = on(dve, lambda e: e.tensor_tensor(place[:, :], bank.t[:, 0:E], running[:, :], ALU.add), point, zeroed_running)
        b = on(dve, lambda e: e.tensor_tensor(place[:, :], place[:, :], onehot[:, t, :], ALU.mult), a)
        counted = on(dve, lambda e: e.tensor_tensor(running[:, :], bank.t[:, E:2 * E], running[:, :], ALU.add), a)
        bank.free = [counted]
        routed.append(t)
        ranked[0] = on(dve, lambda e: e.tensor_reduce(rank[:, t:t + 1], place[:, :], AX.X, ALU.add), b)
        yield

    ranked, routed = [None], []

    def tiles_stream():
        for t in range(T):
            while t not in finished:
                yield
            yield from self_tile(t)

    setting = set_up()
    next(setting)
    tiles = tiles_stream()
    for turn_no, _ in enumerate(cross_stream()):
        for _ in range(2):
            if next(setting, "end") == "end":
                break
        next(tiles, None)
    for _ in setting:
        pass
    for _ in tiles:
        pass

    phase.close()
    last_dve = (done[dve], done[dve].count)
    barrier = [(done[q], done[q].count) for q in (pe, act, dve, pool)] + list(x2_out.values()) + v_dram_free[0] + v_dram_free[1]
    expert_stack = ctx

    ends = sb("ends", [P, E])
    starts = sb("starts", [P, E])
    count_i = sb("count_i", [P, E], I32)
    chosen = sb("chosen", [P, T, E])
    slot = sb("slot", [P, T])
    slot_i = sb("slot_i", [P, T], I32)
    slot_row_i, slot_tile_i = sb("slot_row_i", [P, T], I32), sb("slot_tile_i", [P, T], I32)
    slot_row, slot_tile = sb("slot_row", [P, T]), sb("slot_tile", [P, T])
    in_tile = sb("in_tile", [P, T, SW])
    in_row = [Buffer(sb(f"in_row{i}", [P, P])) for i in range(4)]
    past = sb("past", [P, SW, E])
    of_slot = sb("of_slot", [P, SW])
    weight_row = sb("weight_row", [P, SW])
    ids = sb("ids", [P, SW])
    ids_near = sb("ids_near", [P, SW])
    put_at, take_at = sb("put_at", [P, SW], U32), sb("take_at", [P, SW], U32)
    weight_at, expert_at = sb("weight_at", [P, SW], U32), sb("expert_at", [P, SW], U32)
    NW = 3
    w1 = [Buffer(sb(f"w1_{i}", [P, G, FI])) for i in range(NW)]
    w2 = [Buffer(sb(f"w2_{i}", [P, G, D])) for i in range(NW)]
    b1 = [Buffer(sb(f"b1_{i}", [P, G])) for i in range(NW)]
    b2 = [Buffer(sb(f"b2_{i}", [P, D])) for i in range(NW)]
    rows = [Buffer(sb(f"rows{i}", [P, D])) for i in range(4)]
    normed3 = [Buffer(sb(f"normed3_{i}", [P, D])) for i in range(2)]
    rows_t = [Buffer(sb(f"rows_t{i}", [P, G, P])) for i in range(2)]
    hidden_t = [Buffer(sb(f"hidden_t{i}", [P, G, P])) for i in range(2)]
    for n, w in (("stats", 6), ("mean_var", 2), ("var_eps", 1), ("rstd", 1)):
        for who in ("e0", "e1"):
            small[n, who] = sb(f"{n}_{who}", [P, w])
    for q in (pe, act, dve, pool, sp):
        q.wait(*barrier)

    a = on(dve, lambda e: e.tensor_scalar(count_i[:, :], running[:, :], float(P - 1), None, ALU.add))
    a = on(dve, lambda e: e.tensor_scalar(count_i[:, :], count_i[:, :], 7, None, ALU.arith_shift_right), a)
    a = on(dve, lambda e: e.tensor_copy(starts[:, :], count_i[:, :]), a)
    b = on(dve, lambda e: e.tensor_tensor_scan(ends[:, :], const("ones")[:, 0:E], starts[:, :], 0.0, ALU.mult, ALU.add), a)
    a = on(dve, lambda e: e.tensor_tensor(starts[:, :], ends[:, :], starts[:, :], ALU.subtract), b)
    past_point = on(dve, lambda e: e.tensor_tensor(past[:, :, 0:E - 1], const("iota")[:, 0:SW].unsqueeze(2).broadcast_to([P, SW, E - 1]),
                                      ends[:, 0:E - 1].unsqueeze(1).broadcast_to([P, SW, E - 1]), ALU.is_ge), b)
    c = on(dve, lambda e: e.tensor_reduce(of_slot[:, :], past[:, :, 0:E - 1], AX.X, ALU.add), past_point)
    d = on(dve, lambda e: e.tensor_copy(expert_at[:, :], of_slot[:, :]), c)
    d = on(dve, lambda e: e.scalar_tensor_tensor(out=weight_row[:, :], in0=of_slot[:, :], scalar=float(P), in1=const("row"),
                                                 op0=ALU.mult, op1=ALU.add), c)
    weights_known = on(dve, lambda e: e.tensor_copy(weight_at[:, :], weight_row[:, :]), d)

    w1_rows = ins["L0_ffn_W1"].rearrange("e (p k) n -> (e p) (k n)", k=G)
    w2_rows = ins["L0_ffn_W2"].rearrange("e (p k) n -> (e p) (k n)", k=G)
    b1_rows = ins["L0_ffn_b1"].rearrange("e (p k) -> (e p) k", k=G)
    sig_w = [[signal(f"{n}_gathered{i}") for i in range(NW)] for n in ("w1", "w2", "b1", "b2")]
    sig_rows = [signal(f"rows_gathered{i}") for i in range(4)]
    sig_out = [signal(f"rows_scattered{i}") for i in range(4)]
    w_in, rows_in, put = {}, {}, {}

    def gather(dst, table, index, s, sig, *waits):
        pool.wait(*waits)
        return pool.do(lambda e: e.indirect_dma_start(dst, None, table, bass.IndirectOffsetOnAxis(ap=index[:, s:s + 1], axis=0)), sig, 16)

    def gather_weights(s):
        i = s % NW
        w_in[s] = [gather(w1[i].t[:, :, :].rearrange("p k n -> p (k n)"), w1_rows, weight_at, s, sig_w[0][i], weights_known, *w1[i].free),
                   gather(w2[i].t[:, :, :].rearrange("p k n -> p (k n)"), w2_rows, weight_at, s, sig_w[1][i], weights_known, *w2[i].free),
                   gather(b1[i].t[:, :], b1_rows, weight_at, s, sig_w[2][i], weights_known, *b1[i].free),
                   gather(b2[i].t[:, :], ins["L0_ffn_b2"], expert_at, s, sig_w[3][i], weights_known, *b2[i].free)]

    def gather_rows(s):
        i = s % 4
        rows_in[s] = gather(rows[i].t[:, :], x2_dram[:, :], take_at, s, sig_rows[i], tokens_known, *rows[i].free)

    gather_weights(0)
    gather_weights(1)
    a = on(dve, lambda e: e.tensor_scalar(starts[:, :], starts[:, :], float(P), None, ALU.mult), a)
    a = on(dve, lambda e: e.tensor_tensor(chosen[:, :, :], onehot[:, :, :], starts[:, :].unsqueeze(1).broadcast_to([P, T, E]), ALU.mult), a)
    a = on(dve, lambda e: e.tensor_reduce(slot[:, :], chosen[:, :, :], AX.X, ALU.add), a)
    a = on(dve, lambda e: e.tensor_tensor(slot_i[:, :], slot[:, :], rank[:, :], ALU.add), a)
    b = on(dve, lambda e: e.tensor_scalar(slot_row_i[:, :], slot_i[:, :], P - 1, None, ALU.bitwise_and), a)
    c = on(dve, lambda e: e.tensor_scalar(slot_tile_i[:, :], slot_i[:, :], 7, None, ALU.arith_shift_right), a)
    b = on(dve, lambda e: e.tensor_copy(slot_row[:, :], slot_row_i[:, :]), b)
    c = on(dve, lambda e: e.tensor_copy(slot_tile[:, :], slot_tile_i[:, :]), c)
    c = on(dve, lambda e: e.tensor_tensor(in_tile[:, :, :], const("iota")[:, 0:SW].unsqueeze(1).broadcast_to([P, T, SW]),
                                          slot_tile[:, :].unsqueeze(2).broadcast_to([P, T, SW]), ALU.is_equal), c)
    bank = self_banks[0]
    for t in range(T):
        buf = in_row[t % 4]
        r = on(dve, lambda e, t=t, buf=buf: e.tensor_scalar(buf.t[:, :], const("iota"), slot_row[:, t:t + 1], const("token")[:, t:t + 1],
                                                            ALU.is_equal, ALU.mult), b, *buf.free)
        point = on(pe, lambda e, t=t, buf=buf: e.matmul(bank.t[:, 0:SW], buf.t[:, :], in_tile[:, t, :], start=(t == 0), stop=(t == T - 1)), r, c)
        buf.free = [point]
    a = on(dve, lambda e: e.tensor_scalar(ids[:, :], bank.t[:, 0:SW], float(BIG), None, ALU.add), point)
    bank.free = [a]
    a = on(dve, lambda e: e.tensor_copy(put_at[:, :], ids[:, :]), a)
    a = on(dve, lambda e: e.tensor_scalar(ids_near[:, :], ids[:, :], float(B * S - 1), None, ALU.min), a)
    tokens_known = on(dve, lambda e: e.tensor_copy(take_at[:, :], ids_near[:, :]), a)
    out_rows = out.rearrange("b s d -> (b s) d")

    for s in range(3):
        gather_rows(s)
    gather_weights(2)

    xt = {}

    def prepare(s):
        i, h = s % 4, s % 2
        point = layer_norm(rows[i].t[:, :], rows_in[s], normed3[h], f"e{h}")
        bank = turn_banks[h]
        turned = turn(normed3[h].t, point, bank, stride=G)
        normed3[h].free = [turned]
        moved = on(act, lambda e: e.activation(rows_t[h].t[:, :, :].rearrange("p g n -> p (g n)"), bank.t[:, :], ACT.Copy),
                   turned, *rows_t[h].free)
        bank.free = [moved]
        xt[s] = moved

    prepare(0)
    for s in range(SLOTS):
        i, h, w = s % 4, s % 2, s % NW
        bank = score_banks[h]
        pe.wait(xt[s], w_in[s][0], *bank.free)
        w1_cols = w1[w].t[:, :, :].rearrange("p k (q m) -> p k m q", m=G)
        for m in range(G):
            for kk in range(G):
                point = on(pe, lambda e, m=m, kk=kk, bank=bank, w1_cols=w1_cols, h=h: e.matmul(
                    bank.t[:, m * P:(m + 1) * P], w1_cols[:, kk, m, :], rows_t[h].t[:, kk, :], start=(kk == 0), stop=(kk == G - 1)))
        rows_t[h].free, w1[w].free = [point], [point]
        act.wait(point, w_in[s][2], *hidden_t[h].free)
        for m in range(G):
            g = on(act, lambda e, m=m, bank=bank, h=h, w=w: e.activation(
                hidden_t[h].t[:, m, :], bank.t[:, m * P:(m + 1) * P], ACT.Gelu, bias=b1[w].t[:, m:m + 1]))
        bank.free, b1[w].free = [g], [g]
        if s + 1 < SLOTS:
            prepare(s + 1)
        bank = self_banks[s % 2]
        pe.wait(g, w_in[s][1], *bank.free)
        for m in range(G):
            point = on(pe, lambda e, m=m, bank=bank, h=h, w=w: e.matmul(bank.t[:, :], hidden_t[h].t[:, m, :], w2[w].t[:, m, :],
                                                      start=(m == 0), stop=(m == G - 1)))
        hidden_t[h].free, w2[w].free = [point], [point]
        biased = on(pool, lambda e, i=i, w=w: e.tensor_tensor(rows[i].t[:, :], rows[i].t[:, :], b2[w].t[:, :], ALU.add),
                    w_in[s][3], rows_in[s], xt[s])
        b2[w].free = [biased]
        summed = on(dve, lambda e, i=i, bank=bank: e.tensor_tensor(rows[i].t[:, :], rows[i].t[:, :], bank.t[:, :], ALU.add), biased, point)
        bank.free = [summed]
        pool.wait(summed)
        put[s] = pool.do(lambda e, s=s, i=i: e.indirect_dma_start(
            out_rows, bass.IndirectOffsetOnAxis(ap=put_at[:, s:s + 1], axis=0), rows[i].t[:, :], None,
            bounds_check=B * S - 1, oob_is_err=False), sig_out[i], 16)
        rows[i].free = [put[s]]
        if s + 3 < SLOTS:
            gather_rows(s + 3)
            gather_weights(s + 3)
    pool.wait(*[put[s] for s in range(SLOTS - 4, SLOTS)])

    ctx.close()


_INS = ["x", "ctx_1024", "L0_xattn_W_out", "L0_xattn_b_out", "L0_attn_Wd_q_w", "L0_attn_Wd_q_b", "L0_attn_Wu_q_w",
        "L0_attn_Wu_q_b", "L0_attn_Wq_r_w", "L0_attn_Wq_r_b", "L0_attn_Wk_r_w", "L0_attn_Wk_r_b", "L0_attn_Wd_kv_w",
        "L0_attn_Wd_kv_b", "L0_attn_Wu_k_w", "L0_attn_Wu_k_b", "L0_attn_Wu_v_w", "L0_attn_Wu_v_b", "L0_attn_Wo_w",
        "L0_attn_Wo_b", "L0_ffn_Wg", "L0_ffn_bg", "L0_ffn_W1", "L0_ffn_b1", "L0_ffn_W2", "L0_ffn_b2"]


def kernel(**inputs):
    import concourse.bacc as bacc
    from concourse.bass_utils import run_bass_kernel_spmd

    nc = bacc.Bacc("TRN2", target_bir_lowering=False, num_devices=1)
    table, const_at = constant_table()
    arrays = {f"in_{n}": np.ascontiguousarray(inputs[n]) for n in _INS}
    arrays["in_const"] = table
    ins = {n[3:]: nc.dram_tensor(n, a.shape, mybir.dt.from_np(a.dtype), kind="ExternalInput").ap() for n, a in arrays.items()}
    out = nc.dram_tensor("out_0", (B, S, D), F32, kind="ExternalOutput").ap()
    x2_dram = nc.dram_tensor("x2_scratch", (B * S, D), F32, kind="Internal").ap()
    v_dram = nc.dram_tensor("v_scratch", (2, P, D), F32, kind="Internal").ap()
    program(nc, ins, out, const_at, x2_dram, v_dram)
    result = run_bass_kernel_spmd(nc, [arrays], core_ids=[0])
    return result.results[0]["out_0"]
```

```python
from contextlib import ExitStack

import numpy as np
import concourse.bass as bass
from concourse import mybir

F32, F32R = mybir.dt.float32, mybir.dt.float32r
I32, U32 = mybir.dt.int32, mybir.dt.uint32
ALU, ACT, AX = mybir.AluOpType, mybir.ActivationFunctionType, mybir.AxisListType

P = 128
B, S, D = 64, 32, 512
J = 257
H, HD = 16, 32
G, HL = D // P, P // HD
BT = P // S
T = B * S // P
C2 = (J - 1) // P
DQ = 256
E, FI = 8, 512
SLOTS = T + E - 1
SW = 24
Q_PART, KV_PART = range(0, 2), range(2, 4)
BIG = 4096
EPS = 1e-5
XSCALE = float(HD) ** -0.5
SSCALE = float(1.0 / np.sqrt(np.float32(H + DQ + DQ)))


def constant_table():
    p = np.arange(P)
    pos = (p % S).astype(np.float32)[:, None]
    ids = np.arange(D // 2, dtype=np.float32)
    theta = np.power(np.float32(10000.0), np.float32(-2.0) * ids) / np.float32(D // 2)
    angle = (pos * theta[None, :]).astype(np.float32)
    cos, sin = np.cos(angle).astype(np.float32), np.sin(angle).astype(np.float32)
    parts = {
        "ident": np.eye(P),
        "samehead": (p[:, None] // HD == p[None, :] // HD),
        "latent": (p[:, None] % S == np.arange(S)[None, :]),
        "before": (p[:, None] < p[None, :]),
        "ones": np.ones((P, P)),
        "cos": np.repeat(cos, 2, axis=1),
        "sin": np.stack([-sin, sin], axis=-1).reshape(P, D),
        "iota": np.tile(np.arange(P), (P, 1)),
        "token": p[:, None] + P * np.arange(T)[None, :] - BIG,
        "row": np.repeat(p[:, None], SW, axis=1),
        "minushalf": np.full((P, 1), -0.5),
    }
    at, start = {}, 0
    for name, a in parts.items():
        at[name] = (start, start + a.shape[1])
        start += a.shape[1]
    return np.concatenate([a.astype(np.float32) for a in parts.values()], axis=1), at


class Signal:

    def __init__(self, handle):
        self.handle, self.count = handle, 0


class Queue:

    def __init__(self, engine):
        self.engine, self.passed = engine, {}

    def wait(self, *points):
        for signal, value in points:
            if self.passed.get(signal, 0) < value:
                self.passed[signal] = value
                self.engine.wait_ge(signal.handle, value)

    def do(self, make, signal, by=1):
        make(self.engine).then_inc(signal.handle, by)
        signal.count += by
        return signal, signal.count


class Buffer:

    def __init__(self, tensor):
        self.t, self.free, self.before = tensor, [], []

    def take(self):
        assert self.free is not None
        self.before, self.free = self.free, None
        return self


def program(nc, ins, out, const_at, x2_dram, v_dram):
    ctx = ExitStack()
    names = {}

    def uniq(name):
        names[name] = names.get(name, 0) + 1
        return name if names[name] == 1 else f"{name}_{names[name]}"

    def signal(name):
        return Signal(ctx.enter_context(nc.semaphore(uniq(name))))

    def sb(name, shape, dt=F32, stack=ctx):
        return stack.enter_context(nc.sbuf_tensor(uniq(name), shape, dt))

    pe, act, dve, pool, sp = (Queue(e) for e in (nc.tensor, nc.scalar, nc.vector, nc.gpsimd, nc.sync))
    done = {q: signal(n) for q, n in ((pe, "pe_done"), (act, "act_done"), (dve, "dve_done"), (pool, "pool_done"))}

    def on(queue, make, *waits):
        queue.wait(*waits)
        return queue.do(make, done[queue])

    consts = sb("consts", [P, const_at["minushalf"][1]])

    def const(name):
        a, b = const_at[name]
        return consts[:, a:b]

    ident, samehead, latent = const("ident"), const("samehead"), const("latent")
    cos, sin = const("cos"), const("sin")
    last_t = sb("last_t", [P, G, B])
    running = sb("running", [P, E])
    onehot = sb("onehot", [P, T, E])
    rank = sb("rank", [P, T])
    phase = ExitStack()

    def sba(name, shape, dt=F32):
        return sb(name, shape, dt, phase)

    bias = {n: sba(f"bias_{n}", [P, D]) for n in ("xout", "q", "k", "out")}
    bias_g = sba("bias_g", [P, E])
    wg = sba("wg", [P, G, E])
    weight = {n: (sba(f"{n}_hi", [P, k, D], F32R), sba(f"{n}_lo", [P, k, D], F32R))
              for n, k in (("xout", 4), ("ct", 4), ("qr", 2), ("qc", 2), ("kr", 4), ("kc", 2), ("v", 2), ("out", 4))}

    x_tile = [Buffer(sba(f"x{i}", [P, D])) for i in range(4)]
    context = [Buffer(sba(f"context{i}", [P, C2, D])) for i in range(3)]
    k_t = [Buffer(sba(f"k_t{i}", [P, 2, J])) for i in range(3)]
    prob = [Buffer(sba(f"prob{i}", [P, 2, J])) for i in range(3)]
    prob_t = [Buffer(sba(f"prob_t{i}", [P, 2, C2, P])) for i in range(3)]
    qblock = Buffer(sba("qblock", [P, BT, G, HL, S]))
    qblock2 = Buffer(sba("qblock2", [P, BT, G, HL, S]))
    vblock = Buffer(sba("vblock", [P, G, BT, HL, HD]))
    negmax = [Buffer(sba(f"negmax{i}", [P, G])) for i in range(2)]
    sums = [Buffer(sba(f"sums{i}", [P, G, BT])) for i in range(2)]
    plast = [Buffer(sba(f"plast{i}", [P, G, BT])) for i in range(2)]
    rsum = Buffer(sba("rsum", [P, G, BT]))
    att_raw = Buffer(sba("att_raw", [P, G, BT, S]))
    lhs = [(Buffer(sba(f"lhs_hi{i}", [P, G, P], F32R)), Buffer(sba(f"lhs_lo{i}", [P, G, P], F32R))) for i in range(3)]
    norm_x = Buffer(sba("norm_x", [P, D]))
    work = [Buffer(sba(f"work{i}", [P, D])) for i in range(5)]
    late = [Buffer(sba(f"late{i}", [P, D])) for i in range(3)]
    small = {}
    for n, w in (("stats", 6), ("mean_var", 2), ("var_eps", 1), ("rstd", 1)):
        for who in ("x", "s", "r"):
            small[n, who] = sba(f"{n}_{who}", [P, w])
    smax, ssum = sba("smax", [P, G, BT]), sba("ssum", [P, G, BT])
    logits, top = sba("logits", [P, E]), sba("top", [P, 8])
    top_at, expert = sba("top_at", [P, 8], U32), sba("expert", [P, 1])
    place = sba("place", [P, E])
    low_bias = sba("low_bias", [P, G])

    psum = [Buffer(ctx.enter_context(nc.psum_tensor(f"bank{i}", [P, 512], F32))) for i in range(8)]
    score_banks, turn_banks, att_bank, self_banks = psum[0:2], psum[2:4], psum[4], psum[5:8]
    taken = {}

    def ring(name, buffers):
        taken[name] = taken.get(name, 0) + 1
        return buffers[(taken[name] - 1) % len(buffers)].take()

    s_const = signal("const_loaded")
    const_in = sp.do(lambda e: e.dma_start(consts[:, :], ins["const"]), s_const, 16)
    s_x = [signal(f"x_loaded{i}") for i in range(len(x_tile))]
    s_context = [signal(f"context_loaded{i}") for i in range(len(context))]
    x_rows = ins["x"].rearrange("b s d -> (b s) d").rearrange("(t p) d -> t p d", p=P)
    x_in, context_in = {}, {}

    def load_x(t):
        buf = x_tile[t % len(x_tile)].take()
        sp.wait(*buf.before)
        x_in[t] = sp.do(lambda e: e.dma_start(buf.t[:, :], x_rows[t]), s_x[t % len(x_tile)], 16)

    def load_context(b):
        buf = context[b % len(context)].take()
        sp.wait(*buf.before)
        src = ins["ctx_1024"][b, 0:C2 * P, :].rearrange("(p c) d -> p c d", c=C2)
        context_in[b] = sp.do(lambda e: e.dma_start(buf.t[:, :, :], src), s_context[b % len(context)], 16)

    zeroed_qblock = on(pool, lambda e: e.memset(qblock.t[:, :, :, :, :], 0.0))
    zeroed_running = on(pool, lambda e: e.memset(running[:, :], 0.0))
    load_x(0)
    load_context(0)
    load_context(1)
    last_rows = late[0].take()
    s_last = signal("last_rows_loaded")
    last_in = sp.do(lambda e: e.dma_start(last_rows.t[0:B, :], ins["ctx_1024"][:, J - 1, :]), s_last, 16)
    load_context(2)
    ready = {}

    def halves(t):
        return t[:, :].rearrange("p (i o) -> p i o", o=2)

    def broadcast(dst, name):
        s, src = signal(f"{name}_loaded"), ins[name]
        return act.do(lambda e: e.dma_start(dst, src.unsqueeze(0).broadcast_to([P, src.shape[0]])), s, 16)

    def swap_times_sin(dst, src):
        for o in range(2):
            point = on(dve, lambda e: e.tensor_tensor(halves(dst)[:, :, o], halves(src)[:, :, 1 - o], halves(sin)[:, :, o], ALU.mult))
        return point

    def set_up():
        bank = ring("self", self_banks)
        pe.wait(last_in, const_in)
        for g in range(G):
            point = on(pe, lambda e: e.transpose(bank.t[:, g * B:(g + 1) * B], last_rows.t[0:B, g * P:(g + 1) * P],
                                                 ident[0:B, 0:B]))
        last_rows.free = [point]
        ready["last_t"] = on(act, lambda e: e.activation(last_t[:, :, :].rearrange("p g b -> p (g b)"),
                                                         bank.t[:, 0:G * B], ACT.Copy), point)
        bank.free = [ready["last_t"]]
        yield
        ready["bias_xout"] = broadcast(bias["xout"][:, :], "L0_xattn_b_out")
        ready["bias_g"] = broadcast(bias_g[:, :], "L0_ffn_bg")
        s_wg = signal("wg_loaded")
        ready["wg"] = act.do(lambda e: e.dma_start(wg[:, :, :], ins["L0_ffn_Wg"].rearrange("(g p) e -> p g e", p=P)), s_wg, 16)
        s_low = signal("low_bias_loaded")
        for i, name in enumerate(("L0_attn_Wd_q_b", "L0_attn_Wd_kv_b")):
            low_bias_in = act.do(lambda e: e.dma_start(low_bias[:, 2 * i:2 * i + 2], ins[name].rearrange("(c p) -> p c", p=P), allow_slow_non_contiguous=True), s_low, 16)
        yield
        staging = [(qblock2, signal("weight_loaded0")), (vblock, signal("weight_loaded1"))]
        plan = [("xout", [("L0_xattn_W_out", 0)]), ("ct", [("L0_attn_Wd_q_w", 0), ("L0_attn_Wd_kv_w", DQ)]),
                ("kr", [("L0_attn_Wk_r_w", 0)]), ("kc", [("L0_attn_Wu_k_w", 0)]), ("qr", [("L0_attn_Wq_r_w", 0)]),
                ("qc", [("L0_attn_Wu_q_w", 0)]), ("v", [("L0_attn_Wu_v_w", 0)]), ("out", [("L0_attn_Wo_w", 0)])]
        for i, (n, sources) in enumerate(plan):
            buf, s_in = staging[i % 2]
            buf.take()
            stage = buf.t[:, :, :, :, :].rearrange("p a b c d -> p (a b c d)").rearrange("p (k n) -> p k n", k=G)
            sp.wait(*buf.before)
            for name, col in sources:
                w = ins[name]
                k, width = w.shape[0] // P, w.shape[1]
                point = sp.do(lambda e: e.dma_start(stage[:, 0:k, col:col + width], w.rearrange("(k p) n -> p k n", p=P)), s_in, 16)
            hi, lo = weight[n]
            for c in range(k):
                if n == "xout":
                    bank = ring("self", self_banks)
                    pe.wait(point, *bank.before)
                    for o in range(G):
                        read = on(pe, lambda e: e.transpose(bank.t[:, o * P:(o + 1) * P], stage[:, o, c * P:(c + 1) * P], ident))
                    src, src_ready = bank.t[:, :], read
                else:
                    src, src_ready = stage[:, c, :], point
                a = on(act, lambda e: e.activation(hi[:, c, :], src, ACT.Copy), src_ready)
                b = on(dve, lambda e: e.tensor_tensor(lo[:, c, :], src, hi[:, c, :].bitcast(F32), ALU.subtract), a)
                if n == "xout":
                    bank.free = [b]
                yield
            buf.free = [read] if n == "xout" else [b]
            ready[f"w_{n}"] = b
        for z, _ in staging:
            z.take()
            z.free = [on(pool, lambda e: e.memset(z.t[:, :, :, :, :], 0.0), *z.before)]
        yield
        hi, lo = (x.take() for x in lhs[0])
        rows = low_bias[:, :].unsqueeze(2).broadcast_to([P, G, P])
        a = on(act, lambda e: e.activation(hi.t[:, :, :], rows, ACT.Copy), low_bias_in)
        b = on(dve, lambda e: e.tensor_tensor(lo.t[:, :, :], rows, hi.t[:, :, :].bitcast(F32), ALU.subtract), a)
        low = (hi, lo, b)
        yield

        def carried(name, operand, chunks, dst, bias_name):
            act.wait(*dst.before)
            loaded = broadcast(dst.t[:, :], bias_name)
            bank = ring("self", self_banks)
            point = dense(operand, chunks, name, bank)
            point = on(dve, lambda e: e.tensor_tensor(dst.t[:, :], dst.t[:, :], bank.t[:, :], ALU.add), point, loaded)
            bank.free = [point]
            return point

        for n, rot_bias, plain_bias in (("k", "L0_attn_Wk_r_b", "L0_attn_Wu_k_b"), ("q", "L0_attn_Wq_r_b", "L0_attn_Wu_q_b")):
            chunks = Q_PART if n == "q" else KV_PART
            rot, swapped, plain = ring("work", work), ring("work", work), ring("work", work)
            if n == "q":
                point = carried("qr", low, chunks, rot, rot_bias)
            else:
                act.wait(*rot.before)
                point = broadcast(rot.t[:, :], rot_bias)
            plain_point = carried(f"{n}c", low, chunks, plain, plain_bias)
            yield
            a = on(dve, lambda e: e.tensor_tensor(bias[n][:, :], rot.t[:, :], cos, ALU.mult), point)
            dve.wait(*swapped.before)
            b = swap_times_sin(swapped.t, rot.t)
            c = on(dve, lambda e: e.tensor_tensor(bias[n][:, :], bias[n][:, :], swapped.t[:, :], ALU.add), a, b)
            d = on(dve, lambda e: e.tensor_tensor(bias[n][:, :], bias[n][:, :], plain.t[:, :], ALU.add), c, plain_point)
            rot.free, swapped.free, plain.free = [b], [c], [d]
            ready[f"bias_{n}"] = d
            yield
        v_bias = ring("work", work)
        point = carried("v", low, KV_PART, v_bias, "L0_attn_Wu_v_b")
        yield
        bank = ring("self", self_banks)
        turned = turn(v_bias.t, point, bank)
        v_bias.free = [turned]
        operand = split(bank.t[:, :], turned, bank)
        out_bias = ring("work", work)
        point = carried("out", operand, range(G), out_bias, "L0_attn_Wo_b")
        ready["bias_out"] = on(dve, lambda e: e.tensor_copy(bias["out"][:, :], out_bias.t[:, :]), point)
        out_bias.free = [ready["bias_out"]]
        yield

    def layer_norm(x, x_ready, dst, who):
        stats, mv, ve, rstd = (small[n, who] for n in ("stats", "mean_var", "var_eps", "rstd"))
        a = on(dve, lambda e: e.bn_stats(stats[:, :], x), x_ready)
        a = on(dve, lambda e: e.bn_aggr(mv[:, :], stats[:, :]), a)
        b = on(pool, lambda e: e.tensor_scalar(ve[:, :], mv[:, 1:2], EPS, None, ALU.add), a)
        c = on(pool, lambda e: e.tensor_tensor(rstd[:, :], ve[:, :], const("minushalf"), ALU.pow), b, const_in)
        return on(dve, lambda e: e.tensor_scalar(dst.t[:, :], x, mv[:, 0:1], rstd[:, :], ALU.subtract, ALU.mult),
                  c, *dst.before)

    def turn(src, src_ready, bank, stride=1):
        pe.wait(src_ready, const_in, *bank.before)
        for g in range(G):
            part = src[:, g * P:(g + 1) * P] if stride == 1 else src[:, g::stride]
            point = on(pe, lambda e: e.transpose(bank.t[:, g * P:(g + 1) * P], part, ident))
        return point

    def split(src, src_ready, release):
        taken["lhs"] = taken.get("lhs", 0) + 1
        hi, lo = (x.take() for x in lhs[taken["lhs"] % len(lhs)])
        flat = src.rearrange("p (g n) -> p g n", g=G)
        a = on(act, lambda e: e.activation(hi.t[:, :, :], flat, ACT.Copy), src_ready, *hi.before)
        b = on(dve, lambda e: e.tensor_tensor(lo.t[:, :, :], flat, hi.t[:, :, :].bitcast(F32), ALU.subtract), a, *lo.before)
        release.free = [b]
        return hi, lo, b

    def dense(operand, chunks, name, bank):
        hi, lo, point = operand
        w_hi, w_lo = weight[name]
        pe.wait(point, ready[f"w_{name}"], *bank.before)
        for i, c in enumerate(chunks):
            for j, (l, r) in enumerate(((hi, w_hi), (hi, w_lo), (lo, w_hi))):
                point = on(pe, lambda e: e.matmul(bank.t[:, :], l.t[:, c, :], r[:, i, :], start=(i == 0 and j == 0),
                                                  stop=(i == len(chunks) - 1 and j == 2)))
        hi.free, lo.free = [point], [point]
        return point

    def block_diagonal(bank, turned, dst, scale):
        src = bank.t[:, :].rearrange("p (g b i) -> p b g i", g=G, b=BT)
        for hl in range(HL):
            rows = slice(hl * HD, (hl + 1) * HD)
            if hl < HL // 2:
                a = on(act, lambda e: e.activation(dst.t[rows, :, :, hl, :], src[rows], ACT.Copy, scale=scale), turned, *dst.before)
            else:
                b = on(dve, lambda e: e.tensor_scalar(dst.t[rows, :, :, hl, :], src[rows], scale, None, ALU.mult), turned, *dst.before)
        bank.free = [a, b]
        return a, b

    q_ready, k_ready, scored, last_kept, p_ready, raw_ready = {}, {}, {}, {}, {}, {}
    k_of, prob_of, prob_t_of, bank_of, raw_of, sums_of, plast_of = {}, {}, {}, {}, {}, {}, {}

    def normalise_x(t):
        xb = x_tile[t % len(x_tile)]
        norm_ready[t] = layer_norm(xb.t[:, :], x_in[t], norm_x.take(), "x")

    norm_ready = {}

    def place_queries(t):
        bank = ring("turn", turn_banks)
        turned = turn(norm_x.t, norm_ready[t], bank)
        norm_x.free = [turned]
        act.wait(zeroed_qblock)
        dve.wait(zeroed_qblock)
        q_ready[t] = block_diagonal(bank, turned, qblock.take(), XSCALE)

    def turn_context(b, pair):
        buf, kb, bank = context[b % len(context)], ring("k_t", k_t), ring("turn", turn_banks)
        k_of[b, pair] = kb
        pe.wait(context_in[b], const_in, *bank.before)
        for gg in range(2):
            for c in range(C2):
                g = 2 * pair + gg
                point = on(pe, lambda e: e.transpose(bank.t[:, (gg * C2 + c) * P:(gg * C2 + c + 1) * P],
                                                     buf.t[:, c, g * P:(g + 1) * P], ident))
        dst, src = kb.t[:, :, 0:C2 * P], bank.t[:, :].rearrange("p (g n) -> p g n", g=2)
        if pair == 0:
            moved = on(act, lambda e: e.activation(dst, src, ACT.Copy), point, *kb.before)
        else:
            moved = on(dve, lambda e: e.tensor_copy(dst, src), point, *kb.before)
        last = on(pool, lambda e: e.tensor_copy(kb.t[:, :, J - 1], last_t[:, 2 * pair:2 * pair + 2, b]), ready["last_t"], *kb.before)
        k_ready[b, pair] = moved, last
        bank.free = [moved]

    def score(b, g):
        t, bl = divmod(b, BT)
        pair, gg = divmod(g, 2)
        if g == 0 and bl == 0:
            sums_of[t], plast_of[t] = ring("sums", sums), ring("plast", plast)
        if gg == 0:
            prob_of[b, pair] = ring("prob", prob)
        if g == 0:
            negmax_of[b] = ring("negmax", negmax)
        bank, pb, kb, nm, sm = score_banks[g % 2].take(), prob_of[b, pair], k_of[b, pair], negmax_of[b], sums_of[t]
        pe.wait(*q_ready[t], *k_ready[b, pair], *bank.before)
        point = on(pe, lambda e: e.matmul(bank.t[:, 0:J], qblock.t[:, bl, g, :, :], kb.t[:, gg, :], start=True, stop=True))
        if gg == 1:
            kb.free = [point]
        if g == G - 1 and bl == BT - 1:
            qblock.free = [point]
        largest = on(dve, lambda e: e.tensor_reduce(nm.t[:, g:g + 1], bank.t[:, 0:J], AX.X, ALU.max, negate=True),
                     point, *nm.before)
        scored[b, g] = on(act, lambda e: e.activation(pb.t[:, gg, :], bank.t[:, 0:J], ACT.Exp, bias=nm.t[:, g:g + 1],
                                                      accum_out=sm.t[:, g, bl:bl + 1]), largest, *pb.before, *sm.before)
        bank.free = [scored[b, g]]
        if g == G - 1:
            nm.free = [scored[b, g]]
        if gg == 1:
            pl = plast_of[t]
            last_kept[b, pair] = on(pool, lambda e: e.tensor_copy(pl.t[:, 2 * pair:2 * pair + 2, bl], pb.t[:, :, J - 1]),
                                    scored[b, g], *pl.before)

    negmax_of = {}

    def turn_prob(b, pair):
        pb, tb, bank = prob_of[b, pair], ring("prob_t", prob_t), ring("turn", turn_banks)
        prob_t_of[b, pair] = tb
        pe.wait(scored[b, 2 * pair + 1], *bank.before)
        for gg in range(2):
            for c in range(C2):
                point = on(pe, lambda e: e.transpose(bank.t[:, (gg * C2 + c) * P:(gg * C2 + c + 1) * P],
                                                     pb.t[:, gg, c * P:(c + 1) * P], ident))
        pb.free = [point, last_kept[b, pair]]
        dst = tb.t[:, :, :, :].rearrange("p g c n -> p (g c n)")
        if pair == 0:
            moved = on(dve, lambda e: e.tensor_copy(dst, bank.t[:, :]), point, *tb.before)
        else:
            moved = on(act, lambda e: e.activation(dst, bank.t[:, :], ACT.Copy), point, *tb.before)
        p_ready[b, pair] = moved
        bank.free = [moved]

    def attend(b, pair):
        t, bl = divmod(b, BT)
        cb, tb = context[b % len(context)], prob_t_of[b, pair]
        pe.wait(p_ready[b, pair], context_in[b])
        if pair == 0:
            pe.wait(*att_bank.take().before)
        for gg in range(2):
            for c in range(C2):
                g = 2 * pair + gg
                point = on(pe, lambda e: e.matmul(att_bank.t[:, g * P:(g + 1) * P], cb.t[:, c, g * P:(g + 1) * P],
                                                  tb.t[:, gg, c, :], start=(c == 0), stop=(c == C2 - 1)))
        tb.free = [point]
        if pair == 1:
            cb.free = [point]
            if bl == 0:
                raw_of[t] = att_raw.take()
            raw = raw_of[t]
            src = att_bank.t[:, :].rearrange("p (g h i) -> p g h i", g=G, h=HL)
            points = []
            for hl in range(HL):
                rows = slice(hl * HD, (hl + 1) * HD)
                if hl % 2:
                    points.append(on(act, lambda e: e.activation(raw.t[rows, :, bl, :], src[rows, :, hl, :], ACT.Copy), point, *raw.before))
                else:
                    points.append(on(dve, lambda e: e.tensor_copy(raw.t[rows, :, bl, :], src[rows, :, hl, :]), point, *raw.before))
            att_bank.free = points[2:]
            raw_ready[b] = points[2:]
            if b + len(context) < B:
                load_context(b + len(context))

    def cross_stream():
        normalise_x(0)
        place_queries(0)
        for pair in range(2):
            turn_context(0, pair)
        yield
        for b in range(B):
            t, bl = divmod(b, BT)
            score(b, 0)
            yield
            score(b, 1)
            yield
            if b:
                attend(b - 1, 1)
                if bl == 0:
                    finished.append(t - 1)
                yield
            if b + 1 < B:
                turn_context(b + 1, 0)
                yield
            score(b, 2)
            if bl == 1 and t + 1 < T:
                load_x(t + 1)
            yield
            turn_prob(b, 0)
            if bl == 2 and t + 1 < T:
                normalise_x(t + 1)
            yield
            score(b, 3)
            yield
            if b + 1 < B:
                turn_context(b + 1, 1)
                yield
            attend(b, 0)
            yield
            if bl == BT - 1 and t + 1 < T:
                place_queries(t + 1)
                yield
            turn_prob(b, 1)
            yield
        attend(B - 1, 1)
        finished.append(T - 1)

    finished = []
    s_v_out = [signal(f"v_stored{i}") for i in range(2)]
    s_v_in = [signal(f"v_spread{i}") for i in range(HL)]
    v_dram_free = [[], []]
    s_x2 = [signal(f"x2_stored{i}") for i in range(len(x_tile))]
    x2_out, handed = {}, []
    grid4 = lambda t_: t_[:, :].rearrange("p (g b i) -> p g b i", g=G, b=BT)

    def pause(turns):
        for _ in range(turns):
            yield

    def rotate(kind, operand, chunks, plain_operand, plain_chunks):
        bank = ring("self", self_banks)
        point = dense(operand, chunks, f"{kind}r", bank)
        kept, swapped = ring("work", work), ring("work", work)
        a = on(dve, lambda e: e.tensor_tensor(kept.t[:, :], bank.t[:, :], cos, ALU.mult), point, *kept.before)
        dve.wait(*swapped.before)
        b = swap_times_sin(swapped.t, bank.t)
        bank.free = [b]
        b = on(pool, lambda e: e.tensor_tensor(swapped.t[:, :], swapped.t[:, :], bias[kind][:, :], ALU.add), b, ready[f"bias_{kind}"])
        yield
        bank = ring("self", self_banks)
        point = dense(plain_operand, plain_chunks, f"{kind}c", bank)
        a = on(dve, lambda e: e.tensor_tensor(kept.t[:, :], kept.t[:, :], bank.t[:, :], ALU.add), point, a)
        bank.free = [a]
        a = on(pool, lambda e: e.tensor_tensor(kept.t[:, :], kept.t[:, :], swapped.t[:, :], ALU.add), a, b)
        swapped.free = [a]
        yield
        return kept, a

    def project(t):
        k = t % 2
        xb = x_tile[t % len(x_tile)]
        raw, sm, pl = raw_of[t], sums_of[t], plast_of[t]
        x_plus = on(pool, lambda e: e.tensor_tensor(xb.t[:, :], xb.t[:, :], bias["xout"][:, :], ALU.add),
                    ready["bias_xout"], *q_ready[t])
        inv = on(dve, lambda e: e.reciprocal(rsum.t[:, :, :], sm.t[:, :, :]), scored[BT * t + BT - 1, G - 1], *rsum.take().before)
        sm.free = [inv]
        lat = latent.unsqueeze(1).unsqueeze(1).broadcast_to([P, G, BT, S])
        spread = []
        for src, src_ready in ((pl, last_kept[BT * t + BT - 1, 1]), (rsum, inv)):
            per_head, dst = src.t[:, :, :].unsqueeze(3).broadcast_to([P, G, BT, S]), ring("work", work)
            point = on(pool, lambda e: e.tensor_tensor(grid4(dst.t), per_head, lat, ALU.mult), src_ready, const_in, *dst.before)
            src.free = [point]
            spread.append((dst, point))
        yield from pause(4)
        banks = []
        for buf, point in spread:
            bank = ring("self", self_banks)
            point = on(pe, lambda e: e.matmul(bank.t[:, :], samehead, buf.t[:, :], start=True, stop=True), point, *bank.before)
            buf.free = [point]
            banks.append((bank, point))
        att = ring("work", work)
        (bank, point), (bank_inv, point_inv) = banks
        last = last_t[:, :, BT * t:BT * t + BT].unsqueeze(3).broadcast_to([P, G, BT, S])
        a = on(dve, lambda e: e.tensor_tensor(grid4(att.t), grid4(bank.t), last, ALU.mult), point, ready["last_t"], *att.before)
        bank.free = [a]
        a = on(dve, lambda e: e.tensor_tensor(grid4(att.t), grid4(att.t), raw.t[:, :, :, :], ALU.add), a,
               *[p for b in range(BT * t, BT * t + BT) for p in raw_ready[b]])
        raw.free = [a]
        a = on(dve, lambda e: e.tensor_tensor(att.t[:, :], att.t[:, :], bank_inv.t[:, :], ALU.mult), a, point_inv)
        bank_inv.free = [a]
        operand = split(att.t[:, :], a, att)
        yield from pause(4)
        bank = ring("self", self_banks)
        point = dense(operand, range(G), "xout", bank)
        x1 = on(dve, lambda e: e.tensor_tensor(xb.t[:, :], xb.t[:, :], bank.t[:, :], ALU.add), point, x_plus)
        bank.free = [x1]
        norm = ring("work", work)
        point = layer_norm(xb.t[:, :], x1, norm, "s")
        x_plus = on(pool, lambda e: e.tensor_tensor(xb.t[:, :], xb.t[:, :], bias["out"][:, :], ALU.add), point, ready["bias_out"])
        yield from pause(7)
        bank = ring("self", self_banks)
        turned = turn(norm.t, point, bank)
        norm.free = [turned]
        normed = split(bank.t[:, :], turned, bank)
        yield from pause(3)
        bank = ring("self", self_banks)
        point = dense(normed, range(G), "ct", bank)
        low = ring("work", work)
        low_ready = on(act, lambda e: e.activation(low.t[:, :], bank.t[:, :], ACT.Copy), point, *low.before)
        bank.free = [low_ready]
        yield from pause(3)
        bank = ring("self", self_banks)
        turned = turn(low.t, low_ready, bank)
        low.free = [turned]
        low_t = split(bank.t[:, :], turned, bank)
        yield from pause(3)
        k_buf, k_point = yield from rotate("k", normed, range(G), low_t, KV_PART)
        q_buf, q_point = yield from rotate("q", low_t, Q_PART, low_t, Q_PART)
        bank = ring("self", self_banks)
        turned = turn(k_buf.t, k_point, bank)
        k_buf.free = [turned]
        k2_t = ring("work", work)
        k2 = on(act, lambda e: e.activation(k2_t.t[:, :], bank.t[:, :], ACT.Copy), turned, *k2_t.before)
        bank.free = [k2]
        yield from pause(2)
        bank = ring("self", self_banks)
        point = dense(low_t, KV_PART, "v", bank)
        v_buf = ring("work", work)
        v_point = on(act, lambda e: e.activation(v_buf.t[:, :], bank.t[:, :], ACT.Copy), point, *v_buf.before)
        bank.free = [v_point]
        sp.wait(v_point, *v_dram_free[k])
        stored = sp.do(lambda e: e.dma_start(v_dram[k], v_buf.t[:, :]), s_v_out[k], 16)
        v_buf.free = [stored]
        v_stored[t] = stored
        yield from pause(3)
        bank = ring("self", self_banks)
        turned = turn(q_buf.t, q_point, bank)
        q_buf.free = [turned]
        q2 = block_diagonal(bank, turned, qblock2.take(), SSCALE)
        yield from pause(4)
        bank = ring("self", self_banks)
        pe.wait(*q2, k2, *bank.before)
        for g in range(G):
            for bl in range(BT):
                at = (g * BT + bl) * S
                point = on(pe, lambda e: e.matmul(bank.t[:, at:at + S], qblock2.t[:, bl, g, :, :],
                                                  k2_t.t[:, g * P + bl * S:g * P + (bl + 1) * S], start=True, stop=True))
        qblock2.free, k2_t.free = [point], [point]
        soft = ring("late", late)
        a = on(dve, lambda e: e.tensor_reduce(flat16(smax), rows16(bank.t), AX.X, ALU.max), point)
        a = on(dve, lambda e: e.tensor_tensor(rows16(soft.t), rows16(bank.t), per_row(smax), ALU.subtract), a, *soft.before)
        bank.free = [a]
        handed.append((t, soft, a, x_plus))
        yield from pause(1)

    v_stored = {}
    rows16 = lambda t_: t_[:, :].rearrange("p (n j) -> p n j", j=S)
    flat16 = lambda s_: s_[:, :, :].rearrange("p g b -> p (g b)")
    per_row = lambda s_: flat16(s_).unsqueeze(2).broadcast_to([P, G * BT, S])

    def attend_self(t, soft, a, x_plus):
        k = t % 2
        xb = x_tile[t % len(x_tile)]
        vblock.take()
        sp.wait(v_stored[t], *vblock.before)
        v_in = []
        for hl in range(HL):
            src = v_dram[k].rearrange("(b j) (g h d) -> h j g b d", b=BT, g=G, h=HL)[hl]
            v_in.append(sp.do(lambda e: e.dma_start(vblock.t[hl * S:(hl + 1) * S, :, :, hl, :], src), s_v_in[hl], 16))
        v_dram_free[k] = v_in
        a = on(act, lambda e: e.activation(soft.t[:, :], soft.t[:, :], ACT.Exp), a)
        yield from pause(2)
        b = on(dve, lambda e: e.tensor_reduce(flat16(ssum), rows16(soft.t), AX.X, ALU.add), a)
        b = on(dve, lambda e: e.reciprocal(ssum[:, :, :], ssum[:, :, :]), b)
        a = on(pool, lambda e: e.tensor_tensor(rows16(soft.t), rows16(soft.t), per_row(ssum), ALU.mult), b)
        yield from pause(3)
        soft_t = ring("late", late)
        soft_point = on(dve, lambda e: e.transpose(soft_t.t[:, :], soft.t[:, :]), a, *soft_t.before)
        soft.free = [soft_point]
        yield from pause(5)
        bank = ring("self", self_banks)
        pe.wait(soft_point, *v_in, *bank.before)
        for g in range(G):
            for bl in range(BT):
                at = (g * BT + bl) * S
                point = on(pe, lambda e: e.matmul(bank.t[:, at:at + S], vblock.t[:, g, bl, :, :], soft_t.t[:, at:at + S],
                                                  start=True, stop=True))
        vblock.free, soft_t.free = [point], [point]
        operand = split(bank.t[:, :], point, bank)
        yield from pause(4)
        bank = ring("self", self_banks)
        point = dense(operand, range(G), "out", bank)
        x2 = on(dve, lambda e: e.tensor_tensor(xb.t[:, :], xb.t[:, :], bank.t[:, :], ALU.add), point, x_plus)
        bank.free = [x2]
        sp.wait(x2)
        x2_out[t] = sp.do(lambda e: e.dma_start(x2_dram[t * P:(t + 1) * P, :], xb.t[:, :]), s_x2[t % len(x_tile)], 16)
        yield from pause(1)
        norm = ring("late", late)
        point = layer_norm(xb.t[:, :], x2, norm, "r")
        xb.free = [x2_out[t], point]
        yield from pause(6)
        bank = ring("self", self_banks)
        turned = turn(norm.t, point, bank)
        norm.free = [turned]
        x3 = ring("late", late)
        x3_point = on(act, lambda e: e.activation(x3.t[:, :], bank.t[:, :], ACT.Copy), turned, *x3.before)
        bank.free = [x3_point]
        yield from pause(4)
        bank = ring("self", self_banks)
        pe.wait(x3_point, ready["wg"], *bank.before)
        for g in range(G):
            point = on(pe, lambda e: e.matmul(bank.t[:, 0:E], x3.t[:, g * P:(g + 1) * P], wg[:, g, :],
                                              start=(g == 0), stop=(g == G - 1)))
        x3.free = [point]
        a = on(dve, lambda e: e.tensor_tensor(logits[:, :], bank.t[:, 0:E], bias_g[:, :], ALU.add), point, ready["bias_g"])
        bank.free = [a]
        a = on(dve, lambda e: e.max(top[:, :], logits[:, :]), a)
        a = on(dve, lambda e: e.max_index(top_at[:, :], top[:, :], logits[:, :]), a)
        a = on(dve, lambda e: e.tensor_copy(expert[:, :], top_at[:, 0:1]), a)
        hot = on(dve, lambda e: e.tensor_scalar(onehot[:, t, :], const("iota")[:, 0:E], expert[:, :], None, ALU.is_equal), a)
        yield from pause(4)
        bank = ring("self", self_banks)
        pe.wait(hot, *bank.before)
        on(pe, lambda e: e.matmul(bank.t[:, 0:E], const("before"), onehot[:, t, :], start=True, stop=True))
        point = on(pe, lambda e: e.matmul(bank.t[:, E:2 * E], const("ones"), onehot[:, t, :], start=True, stop=True))
        a = on(dve, lambda e: e.tensor_tensor(place[:, :], bank.t[:, 0:E], running[:, :], ALU.add), point, zeroed_running)
        b = on(dve, lambda e: e.tensor_tensor(place[:, :], place[:, :], onehot[:, t, :], ALU.mult), a)
        counted = on(dve, lambda e: e.tensor_tensor(running[:, :], bank.t[:, E:2 * E], running[:, :], ALU.add), a)
        bank.free = [counted]
        on(dve, lambda e: e.tensor_reduce(rank[:, t:t + 1], place[:, :], AX.X, ALU.add), b, counted)
        yield from pause(1)

    def project_stream():
        for t in range(T):
            while t not in finished:
                yield
            yield from project(t)

    def self_stream():
        for t in range(T):
            while len(handed) <= t:
                yield
            yield from attend_self(*handed[t])

    setting, projecting, attending = set_up(), project_stream(), self_stream()
    next(setting)
    for n, _ in enumerate(cross_stream()):
        for _ in range(3):
            next(setting, None)
        next(projecting, None)
        next(attending, None)
    while True:
        more = [next(stream, "end") for stream in (setting, projecting, attending)]
        if more == ["end"] * 3:
            break

    phase.close()
    barrier = [(done[q], done[q].count) for q in (pe, act, dve, pool)] + list(x2_out.values()) + v_dram_free[0] + v_dram_free[1]

    ends, starts = sb("ends", [P, E]), sb("starts", [P, E])
    count_i = sb("count_i", [P, E], I32)
    chosen = sb("chosen", [P, T, E])
    slot, slot_i = sb("slot", [P, T]), sb("slot_i", [P, T], I32)
    slot_row_i, slot_tile_i = sb("slot_row_i", [P, T], I32), sb("slot_tile_i", [P, T], I32)
    slot_row, slot_tile = sb("slot_row", [P, T]), sb("slot_tile", [P, T])
    in_tile = sb("in_tile", [P, T, SW])
    in_row = [Buffer(sb(f"in_row{i}", [P, P])) for i in range(4)]
    past = sb("past", [P, SW, E])
    of_slot, ids, ids_near = sb("of_slot", [P, SW]), sb("ids", [P, SW]), sb("ids_near", [P, SW])
    put_at, take_at, expert_at = sb("put_at", [P, SW], U32), sb("take_at", [P, SW], U32), sb("expert_at", [P, SW], I32)
    NW, NR = 4, 5
    w1 = [Buffer(sb(f"w1_{i}", [P, G, FI])) for i in range(NW)]
    w2 = [Buffer(sb(f"w2_{i}", [P, G, D])) for i in range(NW)]
    b1 = [Buffer(sb(f"b1_{i}", [P, G])) for i in range(NW)]
    b2 = sb("b2", [E, D])
    b2_hi, b2_lo, expert_hot_r = sb("b2_hi", [E, D], F32R), sb("b2_lo", [E, D], F32R), sb("expert_hot_r", [E, SW, P], F32R)
    rows = [Buffer(sb(f"rows{i}", [P, D])) for i in range(NR)]
    normed3 = [Buffer(sb(f"normed3_{i}", [P, D])) for i in range(2)]
    rows_t = [Buffer(sb(f"rows_t{i}", [P, G, P])) for i in range(2)]
    hidden_t = [Buffer(sb(f"hidden_t{i}", [P, G, P])) for i in range(2)]
    for n, w in (("stats", 6), ("mean_var", 2), ("var_eps", 1), ("rstd", 1)):
        for who in ("e0", "e1"):
            small[n, who] = sb(f"{n}_{who}", [P, w])
    for q in (pe, act, dve, pool, sp):
        q.wait(*barrier)
    s_b2 = signal("b2_loaded")
    b2_in = sp.do(lambda e: e.dma_start(b2[:, :], ins["L0_ffn_b2"]), s_b2, 16)

    a = on(dve, lambda e: e.tensor_scalar(count_i[:, :], running[:, :], float(P - 1), None, ALU.add))
    a = on(dve, lambda e: e.tensor_scalar(count_i[:, :], count_i[:, :], 7, None, ALU.arith_shift_right), a)
    a = on(dve, lambda e: e.tensor_copy(starts[:, :], count_i[:, :]), a)
    b = on(dve, lambda e: e.tensor_tensor_scan(ends[:, :], const("ones")[:, 0:E], starts[:, :], 0.0, ALU.mult, ALU.add), a)
    c = on(dve, lambda e: e.tensor_tensor(past[:, :, 0:E - 1], const("iota")[:, 0:SW].unsqueeze(2).broadcast_to([P, SW, E - 1]),
                                          ends[:, 0:E - 1].unsqueeze(1).broadcast_to([P, SW, E - 1]), ALU.is_ge), b)
    c = on(dve, lambda e: e.tensor_reduce(of_slot[:, :], past[:, :, 0:E - 1], AX.X, ALU.add), c)
    experts_known = on(dve, lambda e: e.tensor_copy(expert_at[:, :], of_slot[:, :]), c)
    starts_point = on(dve, lambda e: e.tensor_tensor(starts[:, :], ends[:, :], starts[:, :], ALU.subtract), b)
    s_w1, s_w2, s_b1 = ([signal(f"{n}_loaded{i}") for i in range(NW)] for n in ("w1", "w2", "b1"))
    s_rows = [signal(f"rows_gathered{i}") for i in range(NR)]
    s_put = [signal(f"rows_scattered{i}") for i in range(NR)]
    w_in, rows_in, put = {}, {}, {}

    def load_weights(s):
        i = s % NW
        sp.wait(experts_known)
        at = nc.sync.value_load(expert_at[0:1, s:s + 1], min_val=0, max_val=E - 1)
        loads = []
        for buf, name, sig, view in ((w1[i], "L0_ffn_W1", s_w1[i], lambda w: w.rearrange("e (p k) n -> p e k n", k=G)),
                                     (b1[i], "L0_ffn_b1", s_b1[i], lambda w: w.rearrange("e (p k) -> p e k", k=G)),
                                     (w2[i], "L0_ffn_W2", s_w2[i], lambda w: w.rearrange("e (p k) n -> p e k n", k=G))):
            buf.take()
            sp.wait(*buf.before)
            src = view(ins[name])
            dst = buf.t[:, :] if len(buf.t.shape) == 2 else buf.t[:, :, :]
            loads.append(sp.do(lambda e: e.dma_start(dst.unsqueeze(1), src[:, bass.ds(at, 1)]), sig, 16))
        w_in[s] = loads

    def gather_rows(s):
        i = s % NR
        rows[i].take()
        pool.wait(tokens_known, *rows[i].before)
        rows_in[s] = pool.do(lambda e: e.indirect_dma_start(
            rows[i].t[:, :], None, x2_dram[:, :], bass.IndirectOffsetOnAxis(ap=take_at[:, s:s + 1], axis=0)), s_rows[i], 16)

    for s in range(NW - 1):
        load_weights(s)
    a = on(dve, lambda e: e.tensor_scalar(starts[:, :], starts[:, :], float(P), None, ALU.mult), starts_point)
    a = on(dve, lambda e: e.tensor_tensor(chosen[:, :, :], onehot[:, :, :], starts[:, :].unsqueeze(1).broadcast_to([P, T, E]), ALU.mult), a)
    a = on(dve, lambda e: e.tensor_reduce(slot[:, :], chosen[:, :, :], AX.X, ALU.add), a)
    a = on(dve, lambda e: e.tensor_tensor(slot_i[:, :], slot[:, :], rank[:, :], ALU.add), a)
    b = on(dve, lambda e: e.tensor_scalar(slot_row_i[:, :], slot_i[:, :], P - 1, None, ALU.bitwise_and), a)
    c = on(dve, lambda e: e.tensor_scalar(slot_tile_i[:, :], slot_i[:, :], 7, None, ALU.arith_shift_right), a)
    b = on(dve, lambda e: e.tensor_copy(slot_row[:, :], slot_row_i[:, :]), b)
    c = on(dve, lambda e: e.tensor_copy(slot_tile[:, :], slot_tile_i[:, :]), c)
    c = on(dve, lambda e: e.tensor_tensor(in_tile[:, :, :], const("iota")[:, 0:SW].unsqueeze(1).broadcast_to([P, T, SW]),
                                          slot_tile[:, :].unsqueeze(2).broadcast_to([P, T, SW]), ALU.is_equal), c)
    bank = self_banks[0].take()
    pe.wait(*bank.before)
    for t in range(T):
        buf = in_row[t % 4].take()
        r = on(dve, lambda e: e.tensor_scalar(buf.t[:, :], const("iota"), slot_row[:, t:t + 1], const("token")[:, t:t + 1],
                                              ALU.is_equal, ALU.mult), b, *buf.before)
        point = on(pe, lambda e: e.matmul(bank.t[:, 0:SW], buf.t[:, :], in_tile[:, t, :], start=(t == 0), stop=(t == T - 1)), r, c)
        buf.free = [point]
    a = on(dve, lambda e: e.tensor_scalar(ids[:, :], bank.t[:, 0:SW], float(BIG), None, ALU.add), point)
    bank.free = [a]
    b = on(dve, lambda e: e.tensor_scalar(ids_near[:, :], ids[:, :], float(B * S - 1), None, ALU.min), a)
    tokens_known = on(dve, lambda e: e.tensor_copy(take_at[:, :], ids_near[:, :]), b)
    for s in range(3):
        gather_rows(s)
    put_known = on(dve, lambda e: e.tensor_copy(put_at[:, :], ids[:, :]), a)
    d = on(dve, lambda e: e.tensor_tensor(expert_hot_r[:, :, :], of_slot[0:E, :].unsqueeze(2).broadcast_to([E, SW, P]),
                                           const("row")[0:E, 0:1].unsqueeze(2).broadcast_to([E, SW, P]), ALU.is_equal), experts_known)
    e1 = on(pool, lambda e: e.tensor_copy(b2_hi[:, :], b2[:, :]), b2_in)
    bias2_ready = on(pool, lambda e: e.tensor_tensor(b2_lo[:, :], b2[:, :], b2_hi[:, :].bitcast(F32), ALU.subtract), e1, d)

    out_rows = out.rearrange("b s d -> (b s) d")
    normed, xt = {}, {}

    def normalise_rows(s):
        i, h = s % NR, s % 2
        normed[s] = layer_norm(rows[i].t[:, :], rows_in[s], normed3[h].take(), f"e{h}")

    def turn_rows(s):
        h = s % 2
        bank = turn_banks[h].take()
        turned = turn(normed3[h].t, normed[s], bank, stride=G)
        normed3[h].free = [turned]
        xt[s] = on(act, lambda e: e.activation(rows_t[h].t[:, :, :].rearrange("p g n -> p (g n)"), bank.t[:, :], ACT.Copy),
                   turned, *rows_t[h].take().before)
        bank.free = [xt[s]]

    def scatter(s):
        i = s % NR
        pool.wait(summed[s], put_known)
        put[s] = pool.do(lambda e: e.indirect_dma_start(
            out_rows, bass.IndirectOffsetOnAxis(ap=put_at[:, s:s + 1], axis=0), rows[i].t[:, :], None,
            bounds_check=B * S - 1, oob_is_err=False), s_put[i], 16)
        rows[i].free = [put[s]]

    summed = {}
    normalise_rows(0)
    turn_rows(0)
    normalise_rows(1)
    for s in range(SLOTS):
        i, h, w = s % NR, s % 2, s % NW
        bank = score_banks[h].take()
        pe.wait(xt[s], w_in[s][0], *bank.before)
        w1_cols = w1[w].t[:, :, :].rearrange("p k (q m) -> p k m q", m=G)
        for m in range(G):
            for kk in range(G):
                point = on(pe, lambda e: e.matmul(bank.t[:, m * P:(m + 1) * P], w1_cols[:, kk, m, :], rows_t[h].t[:, kk, :],
                                                  start=(kk == 0), stop=(kk == G - 1)))
        rows_t[h].free, w1[w].free = [point], [point]
        act.wait(point, w_in[s][1], *hidden_t[h].take().before)
        for m in range(G):
            g = on(act, lambda e: e.activation(hidden_t[h].t[:, m, :], bank.t[:, m * P:(m + 1) * P], ACT.Gelu, bias=b1[w].t[:, m:m + 1]))
        bank.free, b1[w].free = [g], [g]
        if s + 1 < SLOTS:
            turn_rows(s + 1)
        if s + 2 < SLOTS:
            normalise_rows(s + 2)
        bank = self_banks[s % 2].take()
        pe.wait(bias2_ready, *bank.before)
        for j, part in enumerate((b2_hi, b2_lo)):
            on(pe, lambda e: e.matmul(bank.t[:, :], expert_hot_r[:, s, :], part[:, :], start=(j == 0), stop=False))
        pe.wait(g, w_in[s][2])
        for m in range(G):
            point = on(pe, lambda e: e.matmul(bank.t[:, :], hidden_t[h].t[:, m, :], w2[w].t[:, m, :], start=False, stop=(m == G - 1)))
        hidden_t[h].free, w2[w].free = [point], [point]
        summed[s] = on(dve, lambda e: e.tensor_tensor(rows[i].t[:, :], rows[i].t[:, :], bank.t[:, :], ALU.add), point)
        bank.free = [summed[s]]
        if s:
            scatter(s - 1)
        if s + 3 < SLOTS:
            gather_rows(s + 3)
        if s + NW - 1 < SLOTS:
            load_weights(s + NW - 1)
    scatter(SLOTS - 1)
    pool.wait(*[put[s] for s in range(SLOTS - NR, SLOTS)])
    ctx.close()


_INS = ["x", "ctx_1024", "L0_xattn_W_out", "L0_xattn_b_out", "L0_attn_Wd_q_w", "L0_attn_Wd_q_b", "L0_attn_Wu_q_w",
        "L0_attn_Wu_q_b", "L0_attn_Wq_r_w", "L0_attn_Wq_r_b", "L0_attn_Wk_r_w", "L0_attn_Wk_r_b", "L0_attn_Wd_kv_w",
        "L0_attn_Wd_kv_b", "L0_attn_Wu_k_w", "L0_attn_Wu_k_b", "L0_attn_Wu_v_w", "L0_attn_Wu_v_b", "L0_attn_Wo_w",
        "L0_attn_Wo_b", "L0_ffn_Wg", "L0_ffn_bg", "L0_ffn_W1", "L0_ffn_b1", "L0_ffn_W2", "L0_ffn_b2"]


def kernel(**inputs):
    import concourse.bacc as bacc
    from concourse.bass_utils import run_bass_kernel_spmd

    nc = bacc.Bacc("TRN2", target_bir_lowering=False, num_devices=1)
    table, const_at = constant_table()
    arrays = {f"in_{n}": np.ascontiguousarray(inputs[n]) for n in _INS}
    arrays["in_const"] = table
    ins = {n[3:]: nc.dram_tensor(n, a.shape, mybir.dt.from_np(a.dtype), kind="ExternalInput").ap() for n, a in arrays.items()}
    out = nc.dram_tensor("out_0", (B, S, D), F32, kind="ExternalOutput").ap()
    x2_dram = nc.dram_tensor("x2_scratch", (B * S, D), F32, kind="Internal").ap()
    v_dram = nc.dram_tensor("v_scratch", (2, P, D), F32, kind="Internal").ap()
    program(nc, ins, out, const_at, x2_dram, v_dram)
    result = run_bass_kernel_spmd(nc, [arrays], core_ids=[0])
    return result.results[0]["out_0"]
```

```python
from contextlib import ExitStack

import numpy as np
import concourse.bass as bass
from concourse import mybir

F32, F32R, BF16 = mybir.dt.float32, mybir.dt.float32r, mybir.dt.bfloat16
I32, U32 = mybir.dt.int32, mybir.dt.uint32
ALU, ACT, AX = mybir.AluOpType, mybir.ActivationFunctionType, mybir.AxisListType

P = 128
B, S, D = 64, 32, 512
J = 257
H, HD = 16, 32
G, HL = D // P, P // HD
BT = P // S
T = B * S // P
C2 = (J - 1) // P
DQ = 256
E, FI = 8, 512
SLOTS = T + E - 1
SW = 24
BURST = 2
EARLY = 1
Q_PART, KV_PART = range(0, 2), range(2, 4)
BIG = 4096
EPS = 1e-5
XSCALE = float(HD) ** -0.5
SSCALE = float(1.0 / np.sqrt(np.float32(H + DQ + DQ)))


def constant_table():
    p = np.arange(P)
    pos = (p % S).astype(np.float32)[:, None]
    ids = np.arange(D // 2, dtype=np.float32)
    theta = np.power(np.float32(10000.0), np.float32(-2.0) * ids) / np.float32(D // 2)
    angle = (pos * theta[None, :]).astype(np.float32)
    cos, sin = np.cos(angle).astype(np.float32), np.sin(angle).astype(np.float32)
    parts = {
        "ident": np.eye(P),
        "ones": np.ones((P, E)),
        "iota": np.tile(np.arange(P), (P, 1)),
        "tile": np.tile(np.arange(T) - BIG // P, (P, 1)),
        "row": p[:, None],
        "minushalf": np.full((P, 1), -0.5),
        "latent": (p[:, None] % S == np.arange(S)[None, :]),
        "cos": np.repeat(cos, 2, axis=1),
        "sin": np.stack([-sin, sin], axis=-1).reshape(P, D),
        "before": (p[:, None] < p[None, :]),
        "all": np.ones((P, P)),
        "samehead": (p[:, None] // HD == p[None, :] // HD),
    }
    at, start = {}, 0
    for name, a in parts.items():
        at[name] = (start, start + a.shape[1])
        start += a.shape[1]
    return np.concatenate([a.astype(np.float32) for a in parts.values()], axis=1), at


class Signal:

    def __init__(self, handle):
        self.handle, self.count = handle, 0


class Queue:

    def __init__(self, engine, about):
        self.engine, self.passed, self.clock, self.about = engine, {}, 0.0, about

    def wait(self, *points):
        for signal, value in points:
            self.clock = max(self.clock, self.about.get((signal, value), 0.0))
            if self.passed.get(signal, 0) < value:
                self.passed[signal] = value
                self.engine.wait_ge(signal.handle, value)

    def do(self, make, signal, by=1):
        make(self.engine).then_inc(signal.handle, by)
        signal.count += by
        return signal, signal.count


class Buffer:

    def __init__(self, tensor):
        self.t, self.free, self.before = tensor, [], []

    def take(self):
        assert self.free is not None
        self.before, self.free = self.free, None
        return self


def program(nc, ins, out, const_at, x2_dram, v_dram):
    ctx = ExitStack()
    names = {}

    def uniq(name):
        names[name] = names.get(name, 0) + 1
        return name if names[name] == 1 else f"{name}_{names[name]}"

    def signal(name):
        return Signal(ctx.enter_context(nc.semaphore(uniq(name))))

    def sb(name, shape, dt=F32, stack=ctx):
        return stack.enter_context(nc.sbuf_tensor(uniq(name), shape, dt))

    about = {}
    pe, act, dve, pool, sp = (Queue(e, about) for e in (nc.tensor, nc.scalar, nc.vector, nc.gpsimd, nc.sync))
    done = {q: signal(n) for q, n in ((pe, "pe_done"), (act, "act_done"), (dve, "dve_done"), (pool, "pool_done"))}

    usual = {pe: 0.22, act: 0.5, dve: 0.6, pool: 1.2}
    HOP, DMA_US = 0.1, 3.0

    def expected(points):
        return max([about.get(point, 0.0) for point in points], default=0.0)

    def on(queue, make, *waits, us=None):
        queue.wait(*waits)
        queue.clock = max(queue.clock, expected(waits)) + (us or usual[queue])
        point = queue.do(make, done[queue])
        about[point] = queue.clock + HOP
        return point

    def fetch(make, signal, *waits):
        sp.wait(*waits)
        sp.clock = max(sp.clock, expected(waits)) + HOP
        point = sp.do(make, signal, 16)
        about[point] = sp.clock + DMA_US
        return point

    kept_columns = const_at["minushalf"][1]
    consts = sb("consts", [P, kept_columns])
    running = sb("running", [P, E])
    onehot = sb("onehot", [P, T, E])
    rank = sb("rank", [P, T])
    phase = ExitStack()

    def sba(name, shape, dt=F32):
        return sb(name, shape, dt, phase)

    cross_phase = ExitStack()

    far_end = nc.sbuf_top

    def sbx(name, shape, dt=F32):
        return cross_phase.enter_context(nc.sbuf_tensor(uniq(name), shape, dt, side="right"))

    consts_1 = sba("consts_1", [P, const_at["sin"][1] - kept_columns])

    def const(name):
        a, b = const_at[name]
        return consts[:, a:b] if b <= kept_columns else consts_1[:, a - kept_columns:b - kept_columns]

    ident, latent = const("ident"), const("latent")
    samehead = sba("samehead", [P, P], F32R)
    cos, sin = const("cos"), const("sin")
    last_t = sba("last_t", [P, G, B])

    bias = {n: sba(f"bias_{n}", [P, D]) for n in ("xout", "q", "k", "out")}
    bias_g = sba("bias_g", [P, E])
    wg = sba("wg", [P, G, E])
    weight = {n: (sba(f"{n}_hi", [P, k, D], F32R), sba(f"{n}_lo", [P, k, D], F32R))
              for n, k in (("xout", 4), ("ct", 4), ("qr", 2), ("qc", 2), ("kr", 4), ("kc", 2), ("v", 2), ("out", 4))}

    x_tile = [Buffer(sba(f"x{i}", [P, D])) for i in range(4)]
    context = [Buffer(sbx(f"context{i}", [P, C2, D])) for i in range(4)]
    k_t = [Buffer(sbx(f"k_t{i}", [P, 2, J])) for i in range(2)]
    prob = [Buffer(sbx(f"prob{i}", [P, 2, J])) for i in range(2)]
    prob_t = [Buffer(sbx(f"prob_t{i}", [P, 2, C2, P])) for i in range(2)]
    qblock = Buffer(sbx("qblock", [P, BT, G, HL, S]))
    qblock2 = Buffer(sba("qblock2", [P, BT, G, HL, S]))
    vblock = Buffer(sba("vblock", [P, G, BT, HL, HD]))
    negmax = [Buffer(sba(f"negmax{i}", [P, G])) for i in range(2)]
    sums = [Buffer(sba(f"sums{i}", [P, G, BT])) for i in range(2)]
    plast = [Buffer(sba(f"plast{i}", [P, G, BT])) for i in range(2)]
    att_raw = [Buffer(sba(f"att_raw{i}", [P, G, BT, S])) for i in range(2)]
    norm_x = Buffer(sba("norm_x", [P, D]))
    small = {}
    for n, w in (("stats", 6), ("mean_var", 2), ("rstd", 1)):
        small[n, "x"] = sba(f"{n}_x", [P, w])
    smax, ssum = sba("smax", [P, G, BT]), sba("ssum", [P, G, BT])
    before_and_all = sba("before_and_all", [P, 2, P], BF16)
    chosen_one = sba("chosen_one", [P, E], BF16)
    logits, top = sba("logits", [P, E]), sba("top", [P, 8])
    top_at, expert = sba("top_at", [P, 8], U32), sba("expert", [P, 1])
    low_bias = sba("low_bias", [P, G])

    psum = [Buffer(ctx.enter_context(nc.psum_tensor(f"bank{i}", [P, 512], F32))) for i in range(8)]
    score_banks, turn_banks, att_bank, self_banks = psum[0:2], psum[2:4], psum[4], psum[5:8]
    taken = {}

    def ring(name, buffers):
        taken[name] = taken.get(name, 0) + 1
        return buffers[(taken[name] - 1) % len(buffers)].take()

    class Lane:

        def __init__(self, name, make, n_work, n_late, n_operand, banks):
            self.name, self.banks = name, banks
            self.works = [Buffer(make(f"work_{name}{i}", [P, D])) for i in range(n_work)]
            self.lates = [Buffer(make(f"late_{name}{i}", [P, D])) for i in range(n_late)]
            self.operands = [tuple(Buffer(make(f"operand_{part}_{name}{i}", [P, G, P], F32R)) for part in ("hi", "lo"))
                             for i in range(n_operand)]
            self.per_head = [tuple(Buffer(make(f"per_head_{part}{i}", [P, G, BT])) for part in ("hi", "lo")) for i in range(2)]
            for n, w in (("stats", 6), ("mean_var", 2), ("rstd", 1)):
                for who in ("s", "r"):
                    small[n, who + name] = make(f"{n}_{who}_{name}", [P, w])

        def bank_free(self):
            return self.banks[taken.get(f"bank_{self.name}", 0) % len(self.banks)].free or []

        def bank(self):
            return ring(f"bank_{self.name}", self.banks)

        def work(self):
            return ring(f"work_{self.name}", self.works)

        def late(self):
            return ring(f"late_{self.name}", self.lates)

        def operand(self):
            taken[self.name] = taken.get(self.name, 0) + 1
            return tuple(x.take() for x in self.operands[taken[self.name] % len(self.operands)])

    main = Lane("main", sba, 5, 2, 3, self_banks)

    s_const, s_const_1 = signal("const_loaded"), signal("const_1_loaded")
    s_x = [signal(f"x_loaded{i}") for i in range(len(x_tile))]
    s_context = [signal(f"context_loaded{i}") for i in range(len(context))]
    x_rows = ins["x"].rearrange("b s d -> (b s) d").rearrange("(t p) d -> t p d", p=P)
    x_in, context_in = {}, {}

    def load_x(t):
        buf = x_tile[t % len(x_tile)].take()
        x_in[t] = fetch(lambda e: e.dma_start(buf.t[:, :], x_rows[t]), s_x[t % len(x_tile)], *buf.before)

    def load_context(b):
        buf = context[b % len(context)].take()
        src = ins["ctx_1024"][b, 0:C2 * P, :].rearrange("(p c) d -> p c d", c=C2)
        context_in[b] = fetch(lambda e: e.dma_start(buf.t[:, :, :], src), s_context[b % len(context)], *buf.before)

    zeroed_qblock = on(pool, lambda e: e.memset(qblock.t[:, :, :, :, :], 0.0))
    zeroed_running = on(pool, lambda e: e.memset(running[:, :], 0.0))
    load_x(0)
    const_in = sp.do(lambda e: e.dma_start(consts[:, :], ins["const"][:, 0:kept_columns]), s_const, 16)
    load_context(0)
    last_rows = main.lates[0].take()
    s_last = signal("last_rows_loaded")
    last_in = sp.do(lambda e: e.dma_start(last_rows.t[0:B, :], ins["ctx_1024"][:, J - 1, :]), s_last, 16)
    load_context(1)
    load_context(2)
    load_context(3)
    ready = {}

    def halves(t):
        return t[:, :].rearrange("p (i o) -> p i o", o=2)

    def broadcast(dst, name):
        s, src = signal(f"{name}_loaded"), ins[name]
        return act.do(lambda e: e.dma_start(dst, src.unsqueeze(0).broadcast_to([P, src.shape[0]])), s, 16)

    def swap_times_sin(dst, src):
        for o in range(2):
            point = on(dve, lambda e: e.tensor_tensor(halves(dst)[:, :, o], halves(src)[:, :, 1 - o], halves(sin)[:, :, o], ALU.mult), us=0.34)
        return point

    def set_up():
        bank = main.bank()
        pe.wait(last_in, const_in)
        for g in range(G):
            point = on(pe, lambda e: e.transpose(bank.t[:, g * B:(g + 1) * B], last_rows.t[0:B, g * P:(g + 1) * P],
                                                 ident[0:B, 0:B]), us=0.11)
        last_rows.free = [point]
        ready["last_t"] = on(act, lambda e: e.activation(last_t[:, :, :].rearrange("p g b -> p (g b)"),
                                                         bank.t[:, 0:G * B], ACT.Copy), point)
        bank.free = [ready["last_t"]]
        yield []
        ready["bias_xout"] = broadcast(bias["xout"][:, :], "L0_xattn_b_out")
        ready["bias_g"] = broadcast(bias_g[:, :], "L0_ffn_bg")
        s_wg = signal("wg_loaded")
        ready["wg"] = act.do(lambda e: e.dma_start(wg[:, :, :], ins["L0_ffn_Wg"].rearrange("(g p) e -> p g e", p=P)), s_wg, 16)
        s_low = signal("low_bias_loaded")
        for i, name in enumerate(("L0_attn_Wd_q_b", "L0_attn_Wd_kv_b")):
            low_bias_in = act.do(lambda e: e.dma_start(low_bias[:, 2 * i:2 * i + 2], ins[name].rearrange("(c p) -> p c", p=P), allow_slow_non_contiguous=True), s_low, 16)
        yield []
        staging = [(qblock2, signal("weight_loaded0")), (vblock, signal("weight_loaded1"))]
        plan = [("xout", [("L0_xattn_W_out", 0)]), ("ct", [("L0_attn_Wd_q_w", 0), ("L0_attn_Wd_kv_w", DQ)]),
                ("kr", [("L0_attn_Wk_r_w", 0)]), ("kc", [("L0_attn_Wu_k_w", 0)]), ("qr", [("L0_attn_Wq_r_w", 0)]),
                ("qc", [("L0_attn_Wu_q_w", 0)]), ("v", [("L0_attn_Wu_v_w", 0)]), ("out", [("L0_attn_Wo_w", 0)])]
        loaded = {}

        def load_weight(i):
            buf, s_in = staging[i % 2]
            stage = buf.take().t[:, :, :, :, :].rearrange("p a b c d -> p (a b c d)").rearrange("p (k n) -> p k n", k=G)
            for name, col in plan[i][1]:
                w = ins[name]
                k, width = w.shape[0] // P, w.shape[1]
                loaded[i] = stage, fetch(lambda e: e.dma_start(stage[:, 0:k, col:col + width], w.rearrange("(k p) n -> p k n", p=P)), s_in, *buf.before)
                about[loaded[i][1]] += DMA_US

        load_weight(0)
        load_weight(1)
        ready["const_1"] = sp.do(lambda e: e.dma_start(consts_1[:, :], ins["const"][:, kept_columns:const_at["sin"][1]]), s_const_1, 16)
        a, b = const_at["before"][0], const_at["samehead"][1]
        wide = main.work()
        s_const_2 = signal("const_2_loaded")
        const_2_in = sp.do(lambda e: e.dma_start(wide.t[:, 0:b - a], ins["const"][:, a:b]), s_const_2, 16)
        for i, (n, _) in enumerate(plan):
            hi, lo = weight[n]
            stage, point = loaded[i]
            for c in range(hi.shape[1]):
                yield [point, *main.bank_free()]
                if n == "xout":
                    bank = main.bank()
                    pe.wait(point, *bank.before)
                    for o in range(G):
                        read = on(pe, lambda e: e.transpose(bank.t[:, o * P:(o + 1) * P], stage[:, o, c * P:(c + 1) * P], ident), us=0.11)
                    src, src_ready = bank.t[:, :], read
                else:
                    src, src_ready = stage[:, c, :], point
                a = on(act, lambda e: e.activation(hi[:, c, :], src, ACT.Copy), src_ready)
                b = on(dve, lambda e: e.tensor_tensor(lo[:, c, :], src, hi[:, c, :].bitcast(F32), ALU.subtract), a)
                if n == "xout":
                    bank.free = [b]
            staging[i % 2][0].free = [read] if n == "xout" else [b]
            ready[f"w_{n}"] = b
            if i + 2 < len(plan):
                load_weight(i + 2)
        for buf, _ in staging:
            buf.take()
            buf.free = [on(pool, lambda e: e.memset(buf.t[:, :, :, :, :], 0.0), *buf.before)]
        dve.wait(ready["const_1"])
        ready["before"] = on(dve, lambda e: e.tensor_copy(before_and_all[:, :, :].rearrange("p a b -> p (a b)"), wide.t[:, 0:2 * P]), const_2_in)
        ready["samehead"] = on(dve, lambda e: e.tensor_copy(samehead[:, :], wide.t[:, 2 * P:3 * P]))
        wide.free = [ready["samehead"]]
        yield []
        hi, lo = main.operand()
        rows = low_bias[:, :].unsqueeze(2).broadcast_to([P, G, P])
        a = on(act, lambda e: e.activation(hi.t[:, :, :], rows, ACT.Copy), low_bias_in)
        b = on(dve, lambda e: e.tensor_tensor(lo.t[:, :, :], rows, hi.t[:, :, :].bitcast(F32), ALU.subtract), a)
        low = (hi, lo, b)
        yield []

        def carried(name, operand, chunks, dst, bias_name):
            act.wait(*dst.before)
            loaded = broadcast(dst.t[:, :], bias_name)
            bank = main.bank()
            point = dense(operand, chunks, name, bank)
            point = on(dve, lambda e: e.tensor_tensor(dst.t[:, :], dst.t[:, :], bank.t[:, :], ALU.add), point, loaded)
            bank.free = [point]
            return point

        for n, rot_bias, plain_bias in (("k", "L0_attn_Wk_r_b", "L0_attn_Wu_k_b"), ("q", "L0_attn_Wq_r_b", "L0_attn_Wu_q_b")):
            chunks = Q_PART if n == "q" else KV_PART
            rot, swapped, plain = main.work(), main.work(), main.work()
            if n == "q":
                point = carried("qr", low, chunks, rot, rot_bias)
            else:
                act.wait(*rot.before)
                point = broadcast(rot.t[:, :], rot_bias)
            plain_point = carried(f"{n}c", low, chunks, plain, plain_bias)
            yield []
            a = on(dve, lambda e: e.tensor_tensor(bias[n][:, :], rot.t[:, :], cos, ALU.mult), point)
            dve.wait(*swapped.before)
            b = swap_times_sin(swapped.t, rot.t)
            c = on(dve, lambda e: e.tensor_tensor(bias[n][:, :], bias[n][:, :], swapped.t[:, :], ALU.add), a, b)
            d = on(dve, lambda e: e.tensor_tensor(bias[n][:, :], bias[n][:, :], plain.t[:, :], ALU.add), c, plain_point)
            rot.free, swapped.free, plain.free = [b], [c], [d]
            ready[f"bias_{n}"] = d
            yield []
        v_bias = main.work()
        point = carried("v", low, KV_PART, v_bias, "L0_attn_Wu_v_b")
        yield []
        bank = main.bank()
        turned = turn(v_bias.t, point, bank)
        v_bias.free = [turned]
        operand = split(main, bank.t[:, :], turned, bank)
        out_bias = main.work()
        point = carried("out", operand, range(G), out_bias, "L0_attn_Wo_b")
        ready["bias_out"] = on(dve, lambda e: e.tensor_copy(bias["out"][:, :], out_bias.t[:, :]), point)
        out_bias.free = [ready["bias_out"]]
        yield []

    def layer_norm(x, x_ready, dst, who):
        return scale_rows(x, measure_rows(x, x_ready, who), dst, who)

    def measure_rows(x, x_ready, who):
        stats, mv, rstd = (small[n, who] for n in ("stats", "mean_var", "rstd"))
        a = on(dve, lambda e: e.bn_stats(stats[:, :], x), x_ready)
        a = on(dve, lambda e: e.bn_aggr(mv[:, :], stats[:, :]), a, us=0.08)
        b = on(pool, lambda e: e.tensor_scalar(rstd[:, :], mv[:, 1:2], EPS, None, ALU.add), a, us=0.18)
        return on(pool, lambda e: e.tensor_tensor(rstd[:, :], rstd[:, :], const("minushalf"), ALU.pow), b, const_in, us=0.46)

    def scale_rows(x, measured, dst, who):
        mv, rstd = small["mean_var", who], small["rstd", who]
        return on(dve, lambda e: e.tensor_scalar(dst.t[:, :], x, mv[:, 0:1], rstd[:, :], ALU.subtract, ALU.mult),
                  measured, *dst.before)

    def turn(src, src_ready, bank, stride=1):
        pe.wait(src_ready, const_in, *bank.before)
        for g in range(G):
            part = src[:, g * P:(g + 1) * P] if stride == 1 else src[:, g::stride]
            point = on(pe, lambda e: e.transpose(bank.t[:, g * P:(g + 1) * P], part, ident), us=0.11)
        return point

    def split(lane, src, src_ready, release):
        hi, lo = lane.operand()
        flat = src.rearrange("p (g n) -> p g n", g=G)
        a = on(act, lambda e: e.activation(hi.t[:, :, :], flat, ACT.Copy), src_ready, *hi.before)
        b = on(dve, lambda e: e.tensor_tensor(lo.t[:, :, :], flat, hi.t[:, :, :].bitcast(F32), ALU.subtract), a, *lo.before)
        release.free = [b]
        return hi, lo, b

    def dense(operand, chunks, name, bank):
        hi, lo, point = operand
        w_hi, w_lo = weight[name]
        pe.wait(point, ready[f"w_{name}"], *bank.before)
        for i, c in enumerate(chunks):
            for j, (l, r) in enumerate(((hi, w_hi), (hi, w_lo), (lo, w_hi))):
                point = on(pe, lambda e: e.matmul(bank.t[:, :], l.t[:, c, :], r[:, i, :], start=(i == 0 and j == 0),
                                                  stop=(i == len(chunks) - 1 and j == 2)))
        hi.free, lo.free = [point], [point]
        return point

    def block_diagonal(bank, turned, dst, scale):
        src = bank.t[:, :].rearrange("p (g b i) -> p b g i", g=G, b=BT)
        for hl in range(HL):
            rows = slice(hl * HD, (hl + 1) * HD)
            if hl < HL // 2:
                a = on(act, lambda e: e.activation(dst.t[rows, :, :, hl, :], src[rows], ACT.Copy, scale=scale), turned, *dst.before)
            else:
                b = on(dve, lambda e: e.tensor_scalar(dst.t[rows, :, :, hl, :], src[rows], scale, None, ALU.mult), turned, *dst.before)
        bank.free = [a, b]
        return a, b

    q_ready, k_ready, scored, last_kept, p_ready, raw_ready = {}, {}, {}, {}, {}, {}
    k_of, prob_of, prob_t_of, bank_of, raw_of, sums_of, plast_of = {}, {}, {}, {}, {}, {}, {}

    def normalise_x(t):
        xb = x_tile[t % len(x_tile)]
        norm_ready[t] = layer_norm(xb.t[:, :], x_in[t], norm_x.take(), "x")

    norm_ready = {}

    def place_queries(t):
        bank = ring("turn", turn_banks)
        turned = turn(norm_x.t, norm_ready[t], bank)
        norm_x.free = [turned]
        act.wait(zeroed_qblock)
        dve.wait(zeroed_qblock)
        q_ready[t] = block_diagonal(bank, turned, qblock.take(), XSCALE)

    def turn_context(b, pair):
        buf, kb, bank = context[b % len(context)], ring("k_t", k_t), ring("turn", turn_banks)
        k_of[b, pair] = kb
        pe.wait(context_in[b], const_in, *bank.before)
        for gg in range(2):
            for c in range(C2):
                g = 2 * pair + gg
                point = on(pe, lambda e: e.transpose(bank.t[:, (gg * C2 + c) * P:(gg * C2 + c + 1) * P],
                                                     buf.t[:, c, g * P:(g + 1) * P], ident), us=0.11)
        dst, src = kb.t[:, :, 0:C2 * P], bank.t[:, :].rearrange("p (g n) -> p g n", g=2)
        if pair == 0:
            moved = on(act, lambda e: e.activation(dst, src, ACT.Copy), point, *kb.before)
        else:
            moved = on(dve, lambda e: e.tensor_copy(dst, src), point, *kb.before)
        last = on(pool, lambda e: e.tensor_copy(kb.t[:, :, J - 1], last_t[:, 2 * pair:2 * pair + 2, b]), ready["last_t"], *kb.before, us=0.13)
        k_ready[b, pair] = moved, last
        bank.free = [moved]

    def score(b, g):
        t, bl = divmod(b, BT)
        pair, gg = divmod(g, 2)
        if g == 0 and bl == 0:
            sums_of[t], plast_of[t] = ring("sums", sums), ring("plast", plast)
        if gg == 0:
            prob_of[b, pair] = ring("prob", prob)
        if g == 0:
            negmax_of[b] = ring("negmax", negmax)
        bank, pb, kb, nm, sm = score_banks[g % 2].take(), prob_of[b, pair], k_of[b, pair], negmax_of[b], sums_of[t]
        pe.wait(*q_ready[t], *k_ready[b, pair], *bank.before)
        point = on(pe, lambda e: e.matmul(bank.t[:, 0:J], qblock.t[:, bl, g, :, :], kb.t[:, gg, :], start=True, stop=True), us=0.44)
        if gg == 1:
            kb.free = [point]
        if g == G - 1 and bl == BT - 1:
            qblock.free = [point]
        largest = on(dve, lambda e: e.tensor_reduce(nm.t[:, g:g + 1], bank.t[:, 0:J], AX.X, ALU.max, negate=True),
                     point, *nm.before, us=0.34)
        scored[b, g] = on(act, lambda e: e.activation(pb.t[:, gg, :], bank.t[:, 0:J], ACT.Exp, bias=nm.t[:, g:g + 1],
                                                      accum_out=sm.t[:, g, bl:bl + 1]), largest, *pb.before, *sm.before, us=0.45)
        bank.free = [scored[b, g]]
        if g == G - 1:
            nm.free = [scored[b, g]]
        if gg == 1:
            pl = plast_of[t]
            last_kept[b, pair] = on(pool, lambda e: e.tensor_copy(pl.t[:, 2 * pair:2 * pair + 2, bl], pb.t[:, :, J - 1]),
                                    scored[b, g], *pl.before, us=0.13)

    negmax_of = {}

    def turn_prob(b, pair):
        pb, tb, bank = prob_of[b, pair], ring("prob_t", prob_t), ring("turn", turn_banks)
        prob_t_of[b, pair] = tb
        pe.wait(scored[b, 2 * pair + 1], *bank.before)
        for gg in range(2):
            for c in range(C2):
                point = on(pe, lambda e: e.transpose(bank.t[:, (gg * C2 + c) * P:(gg * C2 + c + 1) * P],
                                                     pb.t[:, gg, c * P:(c + 1) * P], ident), us=0.11)
        pb.free = [point, last_kept[b, pair]]
        dst = tb.t[:, :, :, :].rearrange("p g c n -> p (g c n)")
        if pair == 0:
            moved = on(dve, lambda e: e.tensor_copy(dst, bank.t[:, :]), point, *tb.before)
        else:
            moved = on(act, lambda e: e.activation(dst, bank.t[:, :], ACT.Copy), point, *tb.before)
        p_ready[b, pair] = moved
        bank.free = [moved]

    def attend(b, pair):
        t, bl = divmod(b, BT)
        cb, tb = context[b % len(context)], prob_t_of[b, pair]
        pe.wait(p_ready[b, pair], context_in[b])
        if pair == 0:
            pe.wait(*att_bank.take().before)
        for gg in range(2):
            for c in range(C2):
                g = 2 * pair + gg
                point = on(pe, lambda e: e.matmul(att_bank.t[:, g * P:(g + 1) * P], cb.t[:, c, g * P:(g + 1) * P],
                                                  tb.t[:, gg, c, :], start=(c == 0), stop=(c == C2 - 1)))
        tb.free = [point]
        if pair == 1:
            cb.free = [point]
            if bl == 0:
                raw_of[t] = ring("att_raw", att_raw)
            raw = raw_of[t]
            src = att_bank.t[:, :].rearrange("p (g h i) -> p g h i", g=G, h=HL)
            points = []
            for hl in range(HL):
                rows = slice(hl * HD, (hl + 1) * HD)
                if hl % 2:
                    points.append(on(act, lambda e: e.activation(raw.t[rows, :, bl, :], src[rows, :, hl, :], ACT.Copy), point, *raw.before, us=0.16))
                else:
                    points.append(on(dve, lambda e: e.tensor_copy(raw.t[rows, :, bl, :], src[rows, :, hl, :]), point, *raw.before, us=0.2))
            att_bank.free = points[2:]
            raw_ready[b] = points[2:]
            if b + len(context) < B:
                load_context(b + len(context))

    def turn_bank_free():
        return turn_banks[taken.get("turn", 0) % 2].free or []

    def cross_stream():
        normalise_x(0)
        place_queries(0)
        for pair in range(2):
            turn_context(0, pair)
        for b in range(B + 1):
            t, bl = divmod(b, BT)
            if b < B:
                for g in range(2):
                    yield [*q_ready[t], *k_ready[b, 0], *score_banks[g].free]
                    score(b, g)
            if b:
                yield [scored[b - 1, 3], *turn_bank_free()]
                turn_prob(b - 1, 1)
                yield [p_ready[b - 1, 0], *att_bank.free]
                attend(b - 1, 0)
            if b + 1 < B:
                yield [context_in[b + 1], *turn_bank_free()]
                turn_context(b + 1, 0)
            if b < B:
                yield [*k_ready[b, 1], *score_banks[0].free]
                score(b, 2)
                if bl == 1 and t + 1 < T:
                    load_x(t + 1)
                yield score_banks[1].free
                score(b, 3)
                yield [scored[b, 1], *turn_bank_free()]
                turn_prob(b, 0)
                if bl == 2 and t + 1 < T:
                    normalise_x(t + 1)
            if bl == BT - 1 and t + 1 < T:
                yield [norm_ready[t + 1], *qblock.free, *turn_bank_free()]
                place_queries(t + 1)
            if b:
                yield [p_ready[b - 1, 1]]
                attend(b - 1, 1)
                if bl == 0:
                    finished.append(t - 1)
            if b + 1 < B:
                yield [context_in[b + 1], *turn_bank_free()]
                turn_context(b + 1, 1)

    finished = []
    s_v_out = [signal(f"v_stored{i}") for i in range(2)]
    s_v_in = [signal(f"v_spread{i}") for i in range(HL)]
    v_dram_free = [[], []]
    s_x2 = [signal(f"x2_stored{i}") for i in range(len(x_tile))]
    x2_out, handed = {}, {}
    grid4 = lambda t_: t_[:, :].rearrange("p (g b i) -> p g b i", g=G, b=BT)

    def rotate(lane, kind, operand, chunks, plain_operand, plain_chunks):
        bank = lane.bank()
        point = dense(operand, chunks, f"{kind}r", bank)
        kept, swapped = lane.work(), lane.work()
        a = on(dve, lambda e: e.tensor_tensor(kept.t[:, :], bank.t[:, :], cos, ALU.mult), point, *kept.before)
        dve.wait(*swapped.before)
        b = swap_times_sin(swapped.t, bank.t)
        bank.free = [b]
        b = on(pool, lambda e: e.tensor_tensor(swapped.t[:, :], swapped.t[:, :], bias[kind][:, :], ALU.add), b, ready[f"bias_{kind}"])
        yield lane.bank_free()
        bank = lane.bank()
        point = dense(plain_operand, plain_chunks, f"{kind}c", bank)
        a = on(dve, lambda e: e.tensor_tensor(kept.t[:, :], kept.t[:, :], bank.t[:, :], ALU.add), point, a)
        bank.free = [a]
        a = on(pool, lambda e: e.tensor_tensor(kept.t[:, :], kept.t[:, :], swapped.t[:, :], ALU.add), a, b)
        swapped.free = [a]
        yield lane.bank_free()
        return kept, a

    def project(t, lane):
        k = t % 2
        xb = x_tile[t % len(x_tile)]
        raw, sm, pl = raw_of[t], sums_of[t], plast_of[t]
        x_plus = on(pool, lambda e: e.tensor_tensor(xb.t[:, :], xb.t[:, :], bias["xout"][:, :], ALU.add),
                    ready["bias_xout"], *q_ready[t])
        inv = on(dve, lambda e: e.reciprocal(sm.t[:, :, :], sm.t[:, :, :]), scored[BT * t + BT - 1, G - 1], us=0.1)
        lat = latent.unsqueeze(1).unsqueeze(1).broadcast_to([P, G, BT, S])
        spread = []
        for src, src_ready, hi, lo in ((pl, last_kept[BT * t + BT - 1, 1], *lane.per_head[0]), (sm, inv, *lane.per_head[1])):
            a = on(act, lambda e: e.activation(hi.t[:, :, :].bitcast(F32R), src.t[:, :, :], ACT.Copy), src_ready, *hi.take().before, us=0.2)
            b = on(dve, lambda e: e.tensor_tensor(lo.t[:, :, :].bitcast(F32R), src.t[:, :, :], hi.t[:, :, :], ALU.subtract), a, *lo.take().before, us=0.1)
            src.free = [b]
            for part, point, dst in zip((hi, lo), (a, b), lane.operand()):
                spread_out = part.t[:, :, :].unsqueeze(3).broadcast_to([P, G, BT, S])
                flat = dst.t[:, :, :].rearrange("p g (b i) -> p g b i", b=BT)
                part.free = [on(pool if part is hi else dve, lambda e: e.tensor_tensor(flat, spread_out, lat, ALU.mult),
                                point, ready["const_1"], *dst.before)]
                spread.append((dst, part.free[0]))
        yield [*[point for _, point in spread], *lane.bank_free()]
        banks = []
        for parts in (spread[0:2], spread[2:4]):
            bank = lane.bank()
            pe.wait(ready["samehead"], *bank.before)
            for j, (buf, point) in enumerate(parts):
                point = on(pe, lambda e: e.matmul(bank.t[:, :], samehead[:, :], buf.t[:, :, :].rearrange("p g n -> p (g n)"),
                                                  start=(j == 0), stop=(j == 1)), point)
                buf.free = [point]
            banks.append((bank, point))
        att = lane.work()
        (bank, point), (bank_inv, point_inv) = banks
        last = last_t[:, :, BT * t:BT * t + BT].unsqueeze(3).broadcast_to([P, G, BT, S])
        a = on(dve, lambda e: e.tensor_tensor(grid4(att.t), grid4(bank.t), last, ALU.mult), point, ready["last_t"], *att.before)
        bank.free = [a]
        a = on(dve, lambda e: e.tensor_tensor(grid4(att.t), grid4(att.t), raw.t[:, :, :, :], ALU.add), a,
               *[p for b in range(BT * t, BT * t + BT) for p in raw_ready[b]])
        raw.free = [a]
        a = on(dve, lambda e: e.tensor_tensor(att.t[:, :], att.t[:, :], bank_inv.t[:, :], ALU.mult), a, point_inv)
        bank_inv.free = [a]
        operand = split(lane, att.t[:, :], a, att)
        yield [operand[2], *lane.bank_free()]
        bank = lane.bank()
        point = dense(operand, range(G), "xout", bank)
        x1 = on(dve, lambda e: e.tensor_tensor(xb.t[:, :], xb.t[:, :], bank.t[:, :], ALU.add), point, x_plus)
        bank.free = [x1]
        norm = lane.work()
        point = layer_norm(xb.t[:, :], x1, norm, f"s{lane.name}")
        x_plus = on(pool, lambda e: e.tensor_tensor(xb.t[:, :], xb.t[:, :], bias["out"][:, :], ALU.add), point, ready["bias_out"])
        yield [point, *lane.bank_free()]
        bank = lane.bank()
        turned = turn(norm.t, point, bank)
        norm.free = [turned]
        normed = split(lane, bank.t[:, :], turned, bank)
        yield [normed[2], *lane.bank_free()]
        bank = lane.bank()
        point = dense(normed, range(G), "ct", bank)
        low = lane.work()
        low_ready = on(act, lambda e: e.activation(low.t[:, :], bank.t[:, :], ACT.Copy), point, *low.before)
        bank.free = [low_ready]
        yield [low_ready, *lane.bank_free()]
        bank = lane.bank()
        turned = turn(low.t, low_ready, bank)
        low.free = [turned]
        low_t = split(lane, bank.t[:, :], turned, bank)
        yield [low_t[2], *lane.bank_free()]
        k_buf, k_point = yield from rotate(lane, "k", normed, range(G), low_t, KV_PART)
        q_buf, q_point = yield from rotate(lane, "q", low_t, Q_PART, low_t, Q_PART)
        yield [k_point, *lane.bank_free()]
        bank = lane.bank()
        turned = turn(k_buf.t, k_point, bank)
        k_buf.free = [turned]
        k2_t = lane.work()
        k2 = on(act, lambda e: e.activation(k2_t.t[:, :], bank.t[:, :], ACT.Copy), turned, *k2_t.before)
        bank.free = [k2]
        yield [*lane.bank_free()]
        bank = lane.bank()
        point = dense(low_t, KV_PART, "v", bank)
        v_buf = lane.work()
        v_point = on(act, lambda e: e.activation(v_buf.t[:, :], bank.t[:, :], ACT.Copy), point, *v_buf.before)
        bank.free = [v_point]
        stored = fetch(lambda e: e.dma_start(v_dram[k], v_buf.t[:, :]), s_v_out[k], v_point, *v_dram_free[k])
        v_buf.free = [stored]
        v_stored[t] = stored
        yield [q_point, *lane.bank_free()]
        bank = lane.bank()
        turned = turn(q_buf.t, q_point, bank)
        q_buf.free = [turned]
        q2 = block_diagonal(bank, turned, qblock2.take(), SSCALE)
        yield [*q2, k2, *lane.bank_free()]
        bank = lane.bank()
        pe.wait(*q2, k2, *bank.before)
        for g in range(G):
            for bl in range(BT):
                at = (g * BT + bl) * S
                point = on(pe, lambda e: e.matmul(bank.t[:, at:at + S], qblock2.t[:, bl, g, :, :],
                                                  k2_t.t[:, g * P + bl * S:g * P + (bl + 1) * S], start=True, stop=True))
            if g % BURST == BURST - 1 and g < G - 1:
                yield []
        qblock2.free, k2_t.free = [point], [point]
        soft = lane.late()
        a = on(dve, lambda e: e.tensor_reduce(flat16(smax), rows16(bank.t), AX.X, ALU.max), point)
        a = on(dve, lambda e: e.tensor_tensor(rows16(soft.t), rows16(bank.t), per_row(smax), ALU.subtract), a, *soft.before)
        bank.free = [a]
        handed[t] = (soft, a, x_plus)

    v_stored = {}
    rows16 = lambda t_: t_[:, :].rearrange("p (n j) -> p n j", j=S)
    flat16 = lambda s_: s_[:, :, :].rearrange("p g b -> p (g b)")
    per_row = lambda s_: flat16(s_).unsqueeze(2).broadcast_to([P, G * BT, S])

    def attend_self(t, lane, soft, a, x_plus):
        k = t % 2
        xb = x_tile[t % len(x_tile)]
        vblock.take()
        v_in = []
        for hl in range(HL):
            src = v_dram[k].rearrange("(b j) (g h d) -> h j g b d", b=BT, g=G, h=HL)[hl]
            v_in.append(fetch(lambda e: e.dma_start(vblock.t[hl * S:(hl + 1) * S, :, :, hl, :], src), s_v_in[hl], v_stored[t], *vblock.before))
        v_dram_free[k] = v_in
        if t == T - 1:
            for e_ in range(EARLY):
                load_expert(e_)
        a = on(act, lambda e: e.activation(soft.t[:, :], soft.t[:, :], ACT.Exp), a)
        yield [a, *lane.bank_free()]
        b = on(dve, lambda e: e.tensor_reduce(flat16(ssum), rows16(soft.t), AX.X, ALU.add), a)
        b = on(dve, lambda e: e.reciprocal(ssum[:, :, :], ssum[:, :, :]), b, us=0.1)
        a = on(pool, lambda e: e.tensor_tensor(rows16(soft.t), rows16(soft.t), per_row(ssum), ALU.mult), b)
        yield [a, *lane.bank_free()]
        soft_t = lane.late()
        soft_point = on(dve, lambda e: e.transpose(soft_t.t[:, :], soft.t[:, :]), a, *soft_t.before)
        soft.free = [soft_point]
        yield [soft_point, *v_in, *lane.bank_free()]
        bank = lane.bank()
        pe.wait(soft_point, *v_in, *bank.before)
        for g in range(G):
            if g and g % BURST == 0:
                yield []
            for bl in range(BT):
                at = (g * BT + bl) * S
                point = on(pe, lambda e: e.matmul(bank.t[:, at:at + S], vblock.t[:, g, bl, :, :], soft_t.t[:, at:at + S],
                                                  start=True, stop=True))
        vblock.free, soft_t.free = [point], [point]
        operand = split(lane, bank.t[:, :], point, bank)
        yield [operand[2], *lane.bank_free()]
        bank = lane.bank()
        point = dense(operand, range(G), "out", bank)
        x2 = on(dve, lambda e: e.tensor_tensor(xb.t[:, :], xb.t[:, :], bank.t[:, :], ALU.add), point, x_plus)
        bank.free = [x2]
        x2_out[t] = fetch(lambda e: e.dma_start(x2_dram[t * P:(t + 1) * P, :], xb.t[:, :]), s_x2[t % len(x_tile)], x2)
        yield [x2, *lane.bank_free()]
        norm = lane.late()
        point = layer_norm(xb.t[:, :], x2, norm, f"r{lane.name}")
        xb.free = [x2_out[t], point]
        yield [point, *lane.bank_free()]
        bank = lane.bank()
        turned = turn(norm.t, point, bank)
        norm.free = [turned]
        x3 = lane.late()
        x3_point = on(act, lambda e: e.activation(x3.t[:, :], bank.t[:, :], ACT.Copy), turned, *x3.before)
        bank.free = [x3_point]
        yield [x3_point, *lane.bank_free()]
        bank = lane.bank()
        pe.wait(x3_point, ready["wg"], *bank.before)
        for g in range(G):
            point = on(pe, lambda e: e.matmul(bank.t[:, 0:E], x3.t[:, g * P:(g + 1) * P], wg[:, g, :],
                                              start=(g == 0), stop=(g == G - 1)))
        x3.free = [point]
        a = on(dve, lambda e: e.tensor_tensor(logits[:, :], bank.t[:, 0:E], bias_g[:, :], ALU.add), point, ready["bias_g"], us=0.1)
        bank.free = [a]
        a = on(dve, lambda e: e.max(top[:, :], logits[:, :]), a, us=0.1)
        a = on(dve, lambda e: e.max_index(top_at[:, :], top[:, :], logits[:, :]), a, us=0.1)
        a = on(dve, lambda e: e.tensor_copy(expert[:, :], top_at[:, 0:1]), a, us=0.1)
        hot = on(dve, lambda e: e.tensor_scalar(chosen_one[:, :], const("iota")[:, 0:E], expert[:, :], None, ALU.is_equal), a, us=0.1)
        on(dve, lambda e: e.tensor_scalar(onehot[:, t, :], const("iota")[:, 0:E], expert[:, :], None, ALU.is_equal), a, us=0.1)
        yield [hot, *lane.bank_free()]
        bank = lane.bank()
        pe.wait(hot, ready["before"], *bank.before)
        on(pe, lambda e: e.matmul(bank.t[:, 0:E], before_and_all[:, 0, :], chosen_one[:, :], start=True, stop=True), us=0.05)
        point = on(pe, lambda e: e.matmul(bank.t[:, E:2 * E], before_and_all[:, 1, :], chosen_one[:, :], start=True, stop=True), us=0.05)
        a = on(dve, lambda e: e.tensor_tensor(logits[:, :], bank.t[:, 0:E], running[:, :], ALU.add), point, zeroed_running, us=0.1)
        b = on(dve, lambda e: e.tensor_tensor(logits[:, :], logits[:, :], onehot[:, t, :], ALU.mult), a, us=0.1)
        counted = on(dve, lambda e: e.tensor_tensor(running[:, :], bank.t[:, E:2 * E], running[:, :], ALU.add), a, us=0.1)
        bank.free = [counted]
        on(dve, lambda e: e.tensor_reduce(rank[:, t:t + 1], logits[:, :], AX.X, ALU.add), b, counted, us=0.1)

    HELD_UNTIL = 600
    SLACK = 0.0

    def project_stream():
        for t in range(T - 1):
            while t not in finished or "bias_out" not in ready or (t == T - 2 and turn_now[0] < HELD_UNTIL):
                yield None
            yield [p for b in range(BT * t, BT * t + BT) for p in raw_ready[b]]
            yield from project(t, main)

    def self_stream():
        for t in range(T - 1):
            while t not in handed:
                yield None
            yield [handed[t][1]]
            yield from attend_self(t, main, *handed[t])

    def side_stream():
        yield from project(T - 1, side[0])
        yield [handed[T - 1][1]]
        yield from attend_self(T - 1, side[0], *handed[T - 1])

    side = []
    wants = {}
    turn_now = [0]

    def interleave(streams, filler=None):
        streams = list(streams)
        while streams:
            for stream in list(streams):
                if wants.get(stream) is None:
                    wants[stream] = next(stream, "end")
                    if wants[stream] == "end":
                        if stream is filler:
                            return
                        streams.remove(stream)
            able = [stream for stream in streams if wants[stream] is not None]
            if not able:
                continue
            if filler:
                able = [stream for stream in able if turn_now[0] >= not_before.get(stream, 0)]
            met = [stream for stream in able if expected(wants[stream]) <= pe.clock + SLACK]
            chosen = met[0] if met else min(able, key=lambda stream: expected(wants[stream]))
            if chosen is filler:
                turn_now[0] += 1
            not_before[chosen] = turn_now[0] + pace.get(chosen, 0)
            wants[chosen] = None
            wants[chosen] = next(chosen, "end")
            if wants[chosen] == "end":
                if chosen is filler:
                    return
                streams.remove(chosen)

    SLAB = 2 * G * FI
    w_all_at = far_end - E * SLAB * 4
    s_expert = [signal(f"expert_loaded{i}") for i in range(E)]
    expert_in, cross_over, w_all = {}, [], []

    def load_expert(e_):
        sp.wait(*cross_over)
        for i, name in enumerate(("L0_ffn_W1", "L0_ffn_W2")):
            expert_in[e_, i] = sp.do(lambda e: e.dma_start(w_all[0][:, E - 1 - e_, i, :, :], ins[name][e_].rearrange("(p k) n -> p k n", k=G)),
                                     s_expert[e_], 16)

    crossing, setting, projecting, attending = cross_stream(), set_up(), project_stream(), self_stream()
    wants[setting] = next(setting)
    pace, not_before = {projecting: 1, attending: 2}, {}
    interleave((attending, projecting, setting, crossing), crossing)
    for buf in (*context, *k_t, *prob, *prob_t, qblock):
        cross_over.extend(buf.free)
    cross_phase.close()
    cross_phase.enter_context(nc.sbuf_tensor(uniq("early_experts"), [P, EARLY * SLAB], F32, side="right"))
    w_all.append(nc.alloc_sbuf_tensor_at("w_all", [P, E, 2, G, FI], F32, offset=w_all_at))
    side.append(Lane("side", sbx, 4, 2, 2, [*score_banks, *turn_banks, att_bank]))
    for buf in (*side[0].works, *side[0].lates, *[x for pair in side[0].operands for x in pair]):
        buf.free = list(cross_over)
    turn_now[0] = HELD_UNTIL
    interleave((side_stream(), attending, projecting))

    phase.close()
    cross_phase.close()
    cross_phase.enter_context(nc.sbuf_tensor(uniq("experts"), [P, E * SLAB], F32, side="right"))
    barrier = [(done[q], done[q].count) for q in (pe, act, dve, pool)] + list(x2_out.values()) + v_dram_free[0] + v_dram_free[1]

    count_i = sb("count_i", [P, E], I32)
    starts, ends, of_slot = sb("starts", [P, E]), sb("ends", [P, E]), sb("of_slot", [P, SW])
    of_slot_i = sb("of_slot_i", [P, SW], I32)
    unread = sb("unread", [P, 1])
    at_i = sb("at_i", [P, SW], I32)
    put_at, take_at = sb("put_at", [P, SW], U32), sb("take_at", [P, SW], U32)
    b1_all = sb("b1_all", [P, E, G])
    b2 = [Buffer(sb(f"b2_{i}", [P, D])) for i in range(2)]
    b1 = [Buffer(sb(f"b1_{i}", [P, G])) for i in range(2)]
    w1 = [Buffer(sb(f"w1_{i}", [P, FI])) for i in range(2 * G)]
    NR = 6
    rows = [Buffer(sb(f"rows{i}", [P, D])) for i in range(NR)]
    normed3 = [Buffer(sb(f"normed3_{i}", [P, D])) for i in range(2)]
    rows_t = [Buffer(sb(f"rows_t{i}", [P, G, P])) for i in range(2)]
    hidden = Buffer(sb("hidden", [P, G, P]))
    hidden_hi, hidden_lo = ([Buffer(sb(f"hidden_{n}{i}", [P, G, P], F32R)) for i in range(2)] for n in ("hi", "lo"))
    for n, w in (("stats", 6), ("mean_var", 2), ("rstd", 1)):
        for who in ("e0", "e1"):
            small[n, who] = sb(f"{n}_{who}", [P, w])
    routing = ExitStack()

    def sbr(name, shape, dt=F32):
        return sb(name, shape, dt, routing)

    chosen, start_tile = sbr("chosen", [P, T, E]), sbr("start_tile", [P, T])
    rank_i, rank_row_i, rank_tile_i = (sbr(n, [P, T], I32) for n in ("rank_i", "rank_row_i", "rank_tile_i"))
    slot_row, slot_tile = sbr("slot_row", [P, T]), sbr("slot_tile", [P, T])
    in_tile = sbr("in_tile", [P, T, SW])
    tile_and_row = sbr("tile_and_row", [P, T, 2, SW], BF16)
    in_row = sbr("in_row", [P, T, P], BF16)
    past = sbr("past", [P, SW, E])
    place_of = sbr("place_of", [P, SW])
    ids_tile, ids, ids_near = sbr("ids_tile", [P, SW]), sbr("ids", [P, SW]), sbr("ids_near", [P, SW])

    for q in (pe, act, dve, pool, sp):
        q.wait(*barrier)
    on(act, lambda e: e.activation(unread[:, :], running[:, 0:1], ACT.Gelu))
    s_b1, s_b2 = signal("b1_loaded"), [signal(f"b2_loaded{i}") for i in range(2)]
    for e_ in range(E):
        b1_in = sp.do(lambda e: e.dma_start(b1_all[:, E - 1 - e_, :], ins["L0_ffn_b1"][e_].rearrange("(p k) -> p k", k=G)), s_b1, 16)

    load_expert(EARLY)

    a = on(dve, lambda e: e.tensor_scalar(count_i[:, :], running[:, :], 1.0, float(P - 1), ALU.max, ALU.add))
    a = on(dve, lambda e: e.tensor_scalar(count_i[:, :], count_i[:, :], 7, None, ALU.arith_shift_right), a)
    a = on(dve, lambda e: e.tensor_copy(starts[:, :], count_i[:, :]), a)
    b = on(dve, lambda e: e.tensor_tensor_scan(ends[:, :], const("ones"), starts[:, :], 0.0, ALU.mult, ALU.add), a)
    a = on(dve, lambda e: e.tensor_tensor(starts[:, :], ends[:, :], starts[:, :], ALU.subtract), b)
    r = on(dve, lambda e: e.tensor_copy(rank_i[:, :], rank[:, :]))
    a = on(dve, lambda e: e.tensor_tensor(chosen[:, :, :], onehot[:, :, :], starts[:, :].unsqueeze(1).broadcast_to([P, T, E]), ALU.mult), a)
    c = on(dve, lambda e: e.tensor_scalar(rank_row_i[:, :], rank_i[:, :], P - 1, None, ALU.bitwise_and), r)
    d = on(dve, lambda e: e.tensor_scalar(rank_tile_i[:, :], rank_i[:, :], 7, None, ALU.arith_shift_right), r)
    a = on(dve, lambda e: e.tensor_reduce(start_tile[:, :], chosen[:, :, :], AX.X, ALU.add), a)
    c = on(dve, lambda e: e.tensor_copy(slot_row[:, :], rank_row_i[:, :]), c)
    d = on(dve, lambda e: e.tensor_copy(slot_tile[:, :], rank_tile_i[:, :]), d)
    row_ready = []

    def place_in_rows(part):
        ts = slice(part * T // 4, (part + 1) * T // 4)
        row_ready.append(on(dve, lambda e: e.tensor_tensor(in_row[:, ts, :], const("iota").unsqueeze(1).broadcast_to([P, T // 4, P]),
                                                           slot_row[:, ts].unsqueeze(2).broadcast_to([P, T // 4, P]), ALU.is_equal), c))

    a = on(dve, lambda e: e.tensor_tensor(slot_tile[:, :], slot_tile[:, :], start_tile[:, :], ALU.add), a, d)
    place_in_rows(0)
    a = on(dve, lambda e: e.tensor_tensor(in_tile[:, :, :], const("iota")[:, 0:SW].unsqueeze(1).broadcast_to([P, T, SW]),
                                          slot_tile[:, :].unsqueeze(2).broadcast_to([P, T, SW]), ALU.is_equal), a)
    r = on(pool, lambda e: e.tensor_tensor(tile_and_row[:, :, 1, :], in_tile[:, :, :],
                                           const("row").unsqueeze(2).broadcast_to([P, T, SW]), ALU.mult), a)
    place_in_rows(1)
    a = on(dve, lambda e: e.tensor_tensor(tile_and_row[:, :, 0, :], in_tile[:, :, :],
                                          const("tile").unsqueeze(2).broadcast_to([P, T, SW]), ALU.mult), a)
    bank = self_banks[0].take()
    pe.wait(a, r, *bank.before)
    for t in range(T):
        if t in (T // 4, T // 2):
            place_in_rows(t // (T // 4) + 1)
        point = on(pe, lambda e: e.matmul(bank.t[:, 0:2 * SW], in_row[:, t, :], tile_and_row[:, t, :, :].rearrange("p a s -> p (a s)"),
                                          start=(t == 0), stop=(t == T - 1)), row_ready[t // (T // 4)])
    a = on(dve, lambda e: e.tensor_scalar(ids_tile[:, :], bank.t[:, 0:SW], float(P), float(BIG), ALU.mult, ALU.add), point)
    a = on(dve, lambda e: e.tensor_tensor(ids[:, :], ids_tile[:, :], bank.t[:, SW:2 * SW], ALU.add), a)
    bank.free = [a]
    b = on(dve, lambda e: e.tensor_scalar(ids_near[:, :], ids[:, :], float(B * S - 1), None, ALU.min), a)
    tokens_known = on(dve, lambda e: e.tensor_copy(take_at[:, :], ids_near[:, :]), b)
    put_known = on(dve, lambda e: e.tensor_copy(put_at[:, :], ids[:, :]), a)
    c = on(dve, lambda e: e.tensor_tensor(past[:, :, 0:E - 1], const("iota")[:, 0:SW].unsqueeze(2).broadcast_to([P, SW, E - 1]),
                                          ends[:, 0:E - 1].unsqueeze(1).broadcast_to([P, SW, E - 1]), ALU.is_ge))
    c = on(dve, lambda e: e.tensor_reduce(of_slot[:, :], past[:, :, 0:E - 1], AX.X, ALU.add), c)
    d = on(dve, lambda e: e.tensor_scalar(place_of[:, :], of_slot[:, :], -1.0, float(E - 1), ALU.mult, ALU.add), c)
    on(dve, lambda e: e.tensor_copy(of_slot_i[:, :], of_slot[:, :]), c)
    experts_known = on(dve, lambda e: e.tensor_copy(at_i[:, :], place_of[:, :]), d)
    routing.close()
    routed = [experts_known, tokens_known, put_known]
    NC = 6
    w2 = [(Buffer(sb(f"w2_hi{i}", [P, D], F32R)), Buffer(sb(f"w2_lo{i}", [P, D], F32R))) for i in range(NC)]
    for hi, lo in w2:
        hi.free, lo.free = routed, routed

    b2_in = {}
    s_rows = [signal(f"rows_gathered{i}") for i in range(NR)]
    s_put = [signal(f"rows_scattered{i}") for i in range(NR)]
    rows_in, put, summed, normed, xt, w1_ready, w2_ready, b1_ready, shifted, measured = ({} for _ in range(10))

    def gather_rows(s):
        i = s % NR
        rows[i].take()
        pool.wait(tokens_known, *rows[i].before)
        rows_in[s] = pool.do(lambda e: e.indirect_dma_start(
            rows[i].t[:, :], None, x2_dram[:, :], bass.IndirectOffsetOnAxis(ap=take_at[:, s:s + 1], axis=0)), s_rows[i], 16)

    def place(queue, s):
        queue.wait(experts_known, expert_in[min(s, E - 1), 1], *[expert_in[e_, 1] for e_ in range(min(s, E - 1))])
        return queue.engine.value_load(at_i[0:1, s:s + 1], min_val=0, max_val=E - 1)

    def weight_copies(s):
        at = {q: place(q, s) for q in (act, dve)}
        h = s % 2
        source = {q: w_all[0][:, bass.ds(at[q], 1), :, :, :] for q in at}
        chunk = lambda q, i, k: source[q][:, 0, i, k, :]
        w1_ready[s] = []
        for k in range(G - 1):
            buf = w1[h * G + k].take()
            w1_ready[s].append(on(act, lambda e: e.activation(buf.t[:, :], chunk(act, 0, k), ACT.Copy), *buf.before))
        buf, bb = w1[h * G + G - 1].take(), b1[h].take()
        w1_ready[s].append(on(dve, lambda e: e.tensor_copy(buf.t[:, :], chunk(dve, 0, G - 1)), *buf.before))
        b1_ready[s] = on(dve, lambda e: e.tensor_copy(bb.t[:, :], b1_all[:, bass.ds(at[dve], 1), :][:, 0, :]), b1_in, *bb.before)

        def split_w2(chunks):
            for k in chunks:
                hi, lo = (x.take() for x in w2[(s * G + k) % NC])
                a = on(act, lambda e: e.activation(hi.t[:, :], chunk(act, 1, k), ACT.Copy), *hi.before)
                w2_ready[s, k] = on(dve, lambda e: e.tensor_tensor(lo.t[:, :], chunk(dve, 1, k), hi.t[:, :].bitcast(F32), ALU.subtract),
                                    a, *lo.before)

        yield
        split_w2(range(G // 2))
        yield
        split_w2(range(G // 2, G))
        yield

    def measure(s):
        measured[s] = measure_rows(rows[s % NR].t[:, :], rows_in[s], f"e{s % 2}")

    def scale(s):
        normed[s] = scale_rows(rows[s % NR].t[:, :], measured[s], normed3[s % 2].take(), f"e{s % 2}")

    def load_bias(s):
        buf = b2[s % 2].take()
        sp.wait(experts_known, *buf.before)
        at = nc.sync.value_load(of_slot_i[0:1, s:s + 1], min_val=0, max_val=E - 1)
        src = ins["L0_ffn_b2"][bass.ds(at, 1), :].unsqueeze(0).broadcast_to([P, 1, D])
        b2_in[s] = sp.do(lambda e: e.dma_start(buf.t[:, :].unsqueeze(1), src), s_b2[s % 2], 16)

    def add_bias(s):
        i = s % NR
        shifted[s] = on(pool, lambda e: e.tensor_tensor(rows[i].t[:, :], rows[i].t[:, :], b2[s % 2].t[:, :], ALU.add), b2_in[s], normed[s])
        b2[s % 2].free = [shifted[s]]

    def turn_rows(s):
        h = s % 2
        bank = turn_banks[h].take()
        turned = turn(normed3[h].t, normed[s], bank, stride=G)
        normed3[h].free = [turned]
        xt[s] = on(act, lambda e: e.activation(rows_t[h].t[:, :, :].rearrange("p g n -> p (g n)"), bank.t[:, :], ACT.Copy),
                   turned, *rows_t[h].take().before)
        bank.free = [xt[s]]

    out_rows = out.rearrange("b s d -> (b s) d")

    def scatter(s):
        i = s % NR
        pool.wait(summed[s], put_known)
        put[s] = pool.do(lambda e: e.indirect_dma_start(
            out_rows, bass.IndirectOffsetOnAxis(ap=put_at[:, s:s + 1], axis=0), rows[i].t[:, :], None,
            bounds_check=B * S - 1, oob_is_err=False), s_put[i], 16)
        rows[i].free = [put[s]]

    LEAD = NR - 2
    for s in range(LEAD):
        gather_rows(s)
    sp.wait(rows_in[0])
    load_bias(0)
    load_expert(EARLY + 1)
    load_bias(1)
    copying = weight_copies(0)
    next(copying)
    measure(0)
    scale(0)
    turn_rows(0)
    next(copying)
    measure(1)
    scale(1)
    add_bias(0)
    for s in range(SLOTS):
        i, h = s % NR, s % 2
        more = s + 1 < SLOTS
        if EARLY + 2 + s < E:
            sp.wait(xt[s])
            load_expert(EARLY + 2 + s)
        next(copying)
        if more:
            copying = weight_copies(s + 1)
            next(copying)
        pe.wait(xt[s], *w1_ready[s])
        of_bank = []
        for m in range(G):
            bank = score_banks[m // 2]
            if m % 2 == 0:
                pe.wait(*bank.take().before)
            for k in range(G):
                cols = w1[h * G + k].t[:, :].rearrange("p (q m) -> p m q", m=G)[:, m, :]
                point = on(pe, lambda e: e.matmul(bank.t[:, m * P:(m + 1) * P], cols, rows_t[h].t[:, k, :],
                                                  start=(k == 0), stop=(k == G - 1)))
            if m % 2:
                of_bank.append(point)
        rows_t[h].free = [point]
        for k in range(G):
            w1[h * G + k].free = [point]
        raw, hi, lo = hidden.take(), hidden_hi[h].take(), hidden_lo[h].take()
        act.wait(b1_ready[s], *raw.before)
        dve.wait(*lo.before)
        h_ready = []
        for m in range(G):
            bank = score_banks[m // 2]
            g = on(act, lambda e: e.activation(raw.t[:, m, :], bank.t[:, m * P:(m + 1) * P], ACT.Gelu, bias=b1[h].t[:, m:m + 1]),
                   of_bank[m // 2])
            bank.free = [g]
            a = on(act, lambda e: e.activation(hi.t[:, m, :], raw.t[:, m, :], ACT.Copy), g, *hi.before)
            h_ready.append(on(dve, lambda e: e.tensor_tensor(lo.t[:, m, :], raw.t[:, m, :], hi.t[:, m, :].bitcast(F32), ALU.subtract), a))
        raw.free, b1[h].free = [h_ready[-1]], [g]
        if more:
            turn_rows(s + 1)
        if s + 2 < SLOTS:
            measure(s + 2)
        if more:
            next(copying)
        if s + 2 < SLOTS:
            scale(s + 2)
        bank = self_banks[s % 2].take()
        pe.wait(*bank.before)
        for m in range(G):
            w_hi, w_lo = w2[(s * G + m) % NC]
            pe.wait(h_ready[m], w2_ready[s, m])
            for j, (l, r) in enumerate(((hi, w_hi), (hi, w_lo), (lo, w_hi))):
                point = on(pe, lambda e: e.matmul(bank.t[:, :], l.t[:, m, :], r.t[:, :],
                                                  start=(m == 0 and j == 0), stop=(m == G - 1 and j == 2)))
            w_hi.free, w_lo.free = [point], [point]
        hi.free, lo.free = [point], [point]
        summed[s] = on(dve, lambda e: e.tensor_tensor(rows[i].t[:, :], rows[i].t[:, :], bank.t[:, :], ALU.add), point, shifted[s])
        bank.free = [summed[s]]
        if more:
            add_bias(s + 1)
        if s + 2 < SLOTS:
            load_bias(s + 2)
        if s:
            scatter(s - 1)
        if s + LEAD < SLOTS:
            gather_rows(s + LEAD)
    scatter(SLOTS - 1)
    pool.wait(*[put[s] for s in range(SLOTS - NR, SLOTS)])
    cross_phase.close()
    ctx.close()


_INS = ["x", "ctx_1024", "L0_xattn_W_out", "L0_xattn_b_out", "L0_attn_Wd_q_w", "L0_attn_Wd_q_b", "L0_attn_Wu_q_w",
        "L0_attn_Wu_q_b", "L0_attn_Wq_r_w", "L0_attn_Wq_r_b", "L0_attn_Wk_r_w", "L0_attn_Wk_r_b", "L0_attn_Wd_kv_w",
        "L0_attn_Wd_kv_b", "L0_attn_Wu_k_w", "L0_attn_Wu_k_b", "L0_attn_Wu_v_w", "L0_attn_Wu_v_b", "L0_attn_Wo_w",
        "L0_attn_Wo_b", "L0_ffn_Wg", "L0_ffn_bg", "L0_ffn_W1", "L0_ffn_b1", "L0_ffn_W2", "L0_ffn_b2"]


def kernel(**inputs):
    import concourse.bacc as bacc
    from concourse.bass_utils import run_bass_kernel_spmd

    nc = bacc.Bacc("TRN2", target_bir_lowering=False, num_devices=1)
    table, const_at = constant_table()
    arrays = {f"in_{n}": np.ascontiguousarray(inputs[n]) for n in _INS}
    arrays["in_const"] = table
    ins = {n[3:]: nc.dram_tensor(n, a.shape, mybir.dt.from_np(a.dtype), kind="ExternalInput").ap() for n, a in arrays.items()}
    out = nc.dram_tensor("out_0", (B, S, D), F32, kind="ExternalOutput").ap()
    x2_dram = nc.dram_tensor("x2_scratch", (B * S, D), F32, kind="Internal").ap()
    v_dram = nc.dram_tensor("v_scratch", (2, P, D), F32, kind="Internal").ap()
    program(nc, ins, out, const_at, x2_dram, v_dram)
    result = run_bass_kernel_spmd(nc, [arrays], core_ids=[0])
    return result.results[0]["out_0"]
```
